# Optimizing a Trainium2 kernel written in Bass

```python
import numpy as np
import jax
import jax.numpy as jnp

def _softmax(x, axis=-1):
    return jax.nn.softmax(x, axis=axis)
def _gelu(x):
    return jax.nn.gelu(x, approximate=True)
def _silu(x):
    return jax.nn.silu(x)
def _sigmoid(x):
    return jax.nn.sigmoid(x)
def _layernorm(x, axis=-1, eps=1e-5):
    m = jnp.mean(x, axis=axis, keepdims=True)
    v = jnp.var(x, axis=axis, keepdims=True)
    return (x - m) / jnp.sqrt(v + eps)
def _scatter_add(tgt, idx, src, axis=0):
    return tgt.at[idx].add(src)
def _segment_sum(src, seg, n):
    return jax.ops.segment_sum(src, seg, n)

kernel_name = 'mk_conv_seq_d2_conv_nchw128_4f1c5e'

def setup_inputs(seed: int = 0):
    np.random.seed(seed)
    _w = jnp.asarray
    def _rec_inputs():
        import jax
        import jax.numpy as jnp
        _gk = jax.random.key(seed)
        x = -0.0005207 + 1.001 * jax.random.normal(jax.random.fold_in(_gk, 1), (4, 128, 64, 64), jnp.float32)
        return x
    x = _rec_inputs()
    def _L0_conv_setup():
        import jax, jax.numpy as jnp
        import numpy as np
        NUM_GROUPS = 32
        EPS = 1e-05

        def group_norm(x, w, b):
            B, C, H, W = x.shape
            xg = x.reshape(B, NUM_GROUPS, -1)
            mean = jnp.mean(xg, axis=-1, keepdims=True)
            var = jnp.var(xg, axis=-1, keepdims=True)
            h = ((xg - mean) * jax.lax.rsqrt(var + EPS)).reshape(B, C, H, W)
            return h * w[None, :, None, None] + b[None, :, None, None]
        key = jax.random.key(seed)
        ks = jax.random.split(key, 3)
        B, C, H, W = (4, 128, 64, 64)
        x = jax.random.normal(ks[0], (B, C, H, W), dtype=jnp.float32)
        norm_w = jnp.ones((C,), jnp.float32)
        norm_b = jnp.zeros((C,), jnp.float32)
        qkv_w = jax.random.normal(ks[1], (3 * C, C), dtype=jnp.float32) * C ** (-0.5)
        qkv_b = jnp.zeros((3 * C,), jnp.float32)
        proj_w = jax.random.normal(ks[2], (C, C), dtype=jnp.float32) * C ** (-0.5)
        proj_b = jnp.zeros((C,), jnp.float32)
        return {'x': x, 'norm_w': norm_w, 'norm_b': norm_b, 'qkv_w': qkv_w, 'qkv_b': qkv_b, 'proj_w': proj_w, 'proj_b': proj_b}
    _L0_conv_all = _L0_conv_setup()
    _L0_conv_in = {k: v for k, v in _L0_conv_all.items() if k in ('norm_w', 'norm_b', 'qkv_w', 'qkv_b', 'proj_w', 'proj_b', )}
    del _L0_conv_all

    def _L1_conv_setup():
        import jax, jax.numpy as jnp
        import numpy as np

        def conv2d(x, w, stride=1, padding=1):
            return jax.lax.conv_general_dilated(x, w, (stride, stride), [(padding, padding)] * 2, dimension_numbers=('NCHW', 'OIHW', 'NCHW'))

        def batchnorm(x, g, b, eps=1e-05):
            m = x.mean(axis=(0, 2, 3), keepdims=True)
            v = x.var(axis=(0, 2, 3), keepdims=True)
            return g[None, :, None, None] * (x - m) * jax.lax.rsqrt(v + eps) + b[None, :, None, None]

        def deform_conv(x, offset, w):
            B, C, H, W = x.shape
            N = 9
            xp = jnp.pad(x, ((0, 0), (0, 0), (1, 1), (1, 1)))
            Hp, Wp = (H + 2, W + 2)
            dn = jnp.arange(-1, 2, dtype=x.dtype)
            pn_x = jnp.repeat(dn, 3)
            pn_y = jnp.tile(dn, 3)
            off = offset.transpose(0, 2, 3, 1)
            px = jnp.arange(1, H + 1, dtype=x.dtype)[None, :, None, None] + pn_x + off[..., :N]
            py = jnp.arange(1, W + 1, dtype=x.dtype)[None, None, :, None] + pn_y + off[..., N:]
            px = jnp.clip(px, 0, Hp - 1)
            py = jnp.clip(py, 0, Wp - 1)
            fx = jnp.floor(jax.lax.stop_gradient(px))
            fy = jnp.floor(jax.lax.stop_gradient(py))
            x0 = jnp.clip(fx, 0, Hp - 1)
            x1 = jnp.clip(fx + 1, 0, Hp - 1)
            y0 = jnp.clip(fy, 0, Wp - 1)
            y1 = jnp.clip(fy + 1, 0, Wp - 1)
            xf = xp.reshape(B, C, Hp * Wp)

            def gather(ix, iy):
                idx = (ix * Wp + iy).astype(jnp.int32).reshape(B, 1, -1)
                return jnp.take_along_axis(xf, idx, axis=2).reshape(B, C, H, W, N)
            g_lt = ((1 + (x0 - px)) * (1 + (y0 - py)))[:, None]
            g_rb = ((1 - (x1 - px)) * (1 - (y1 - py)))[:, None]
            g_lb = ((1 + (x0 - px)) * (1 - (y1 - py)))[:, None]
            g_rt = ((1 - (x1 - px)) * (1 + (y0 - py)))[:, None]
            xo = g_lt * gather(x0, y0) + g_rb * gather(x1, y1) + g_lb * gather(x0, y1) + g_rt * gather(x1, y0)
            xo = xo.reshape(B, C, H, W, 3, 3).transpose(0, 1, 2, 4, 3, 5).reshape(B, C, H * 3, W * 3)
            return jax.lax.conv_general_dilated(xo, w, (3, 3), 'VALID', dimension_numbers=('NCHW', 'OIHW', 'NCHW'))
        key = jax.random.key(seed)
        ks = jax.random.split(key, 4)
        B, Cin, P, H, W = (16, 128, 128, 56, 56)
        return {'x': jax.random.normal(ks[0], (B, Cin, H, W), jnp.float32), 'w1': jax.random.normal(ks[1], (P, Cin, 3, 3), jnp.float32) * 0.05, 'g1': jnp.ones((P,), jnp.float32), 'b1': jnp.zeros((P,), jnp.float32), 'w_off': jax.random.normal(ks[2], (18, P, 3, 3), jnp.float32) * 0.01, 'b_off': jnp.zeros((18,), jnp.float32), 'w2': jax.random.normal(ks[3], (P, P, 3, 3), jnp.float32) * 0.05, 'g2': jnp.ones((P,), jnp.float32), 'b2': jnp.zeros((P,), jnp.float32)}
    _L1_conv_all = _L1_conv_setup()
    _L1_conv_in = {k: v for k, v in _L1_conv_all.items() if k in ('w1', 'g1', 'b1', 'w_off', 'b_off', 'w2', 'g2', 'b2', )}
    del _L1_conv_all

    return {
        "x": x,
        "L0_conv_norm_w": _L0_conv_in["norm_w"],
        "L0_conv_norm_b": _L0_conv_in["norm_b"],
        "L0_conv_qkv_w": _L0_conv_in["qkv_w"],
        "L0_conv_qkv_b": _L0_conv_in["qkv_b"],
        "L0_conv_proj_w": _L0_conv_in["proj_w"],
        "L0_conv_proj_b": _L0_conv_in["proj_b"],
        "L1_conv_w1": _L1_conv_in["w1"],
        "L1_conv_g1": _L1_conv_in["g1"],
        "L1_conv_b1": _L1_conv_in["b1"],
        "L1_conv_w_off": _L1_conv_in["w_off"],
        "L1_conv_b_off": _L1_conv_in["b_off"],
        "L1_conv_w2": _L1_conv_in["w2"],
        "L1_conv_g2": _L1_conv_in["g2"],
        "L1_conv_b2": _L1_conv_in["b2"],
    }

def reference(x, L0_conv_norm_w, L0_conv_norm_b, L0_conv_qkv_w, L0_conv_qkv_b, L0_conv_proj_w, L0_conv_proj_b, L1_conv_w1, L1_conv_g1, L1_conv_b1, L1_conv_w_off, L1_conv_b_off, L1_conv_w2, L1_conv_g2, L1_conv_b2):
    import jax
    import jax.numpy as jnp
    def _L0_conv_ref(x, norm_w, norm_b, qkv_w, qkv_b, proj_w, proj_b):
        import jax, jax.numpy as jnp
        import numpy as np
        NUM_GROUPS = 32
        EPS = 1e-05

        def group_norm(x, w, b):
            B, C, H, W = x.shape
            xg = x.reshape(B, NUM_GROUPS, -1)
            mean = jnp.mean(xg, axis=-1, keepdims=True)
            var = jnp.var(xg, axis=-1, keepdims=True)
            h = ((xg - mean) * jax.lax.rsqrt(var + EPS)).reshape(B, C, H, W)
            return h * w[None, :, None, None] + b[None, :, None, None]
        B, C, H, W = x.shape
        N = H * W
        scale = C ** (-0.5)
        h = group_norm(x, norm_w, norm_b)
        qkv = jnp.einsum('bchw,dc->bdhw', h, qkv_w) + qkv_b[None, :, None, None]
        q, k, v = jnp.split(qkv.reshape(B, 3 * C, N), 3, axis=1)
        attn = jax.nn.softmax(jnp.einsum('bcn,bcm->bnm', q, k) * scale, axis=-1)
        out = jnp.einsum('bnm,bcm->bcn', attn, v).reshape(B, C, H, W)
        out = jnp.einsum('bchw,dc->bdhw', out, proj_w) + proj_b[None, :, None, None]
        return x + out

    def _L1_conv_ref(x, w1, g1, b1, w_off, b_off, w2, g2, b2):
        import jax, jax.numpy as jnp
        import numpy as np

        def conv2d(x, w, stride=1, padding=1):
            return jax.lax.conv_general_dilated(x, w, (stride, stride), [(padding, padding)] * 2, dimension_numbers=('NCHW', 'OIHW', 'NCHW'))

        def batchnorm(x, g, b, eps=1e-05):
            m = x.mean(axis=(0, 2, 3), keepdims=True)
            v = x.var(axis=(0, 2, 3), keepdims=True)
            return g[None, :, None, None] * (x - m) * jax.lax.rsqrt(v + eps) + b[None, :, None, None]

        def deform_conv(x, offset, w):
            B, C, H, W = x.shape
            N = 9
            xp = jnp.pad(x, ((0, 0), (0, 0), (1, 1), (1, 1)))
            Hp, Wp = (H + 2, W + 2)
            dn = jnp.arange(-1, 2, dtype=x.dtype)
            pn_x = jnp.repeat(dn, 3)
            pn_y = jnp.tile(dn, 3)
            off = offset.transpose(0, 2, 3, 1)
            px = jnp.arange(1, H + 1, dtype=x.dtype)[None, :, None, None] + pn_x + off[..., :N]
            py = jnp.arange(1, W + 1, dtype=x.dtype)[None, None, :, None] + pn_y + off[..., N:]
            px = jnp.clip(px, 0, Hp - 1)
            py = jnp.clip(py, 0, Wp - 1)
            fx = jnp.floor(jax.lax.stop_gradient(px))
            fy = jnp.floor(jax.lax.stop_gradient(py))
            x0 = jnp.clip(fx, 0, Hp - 1)
            x1 = jnp.clip(fx + 1, 0, Hp - 1)
            y0 = jnp.clip(fy, 0, Wp - 1)
            y1 = jnp.clip(fy + 1, 0, Wp - 1)
            xf = xp.reshape(B, C, Hp * Wp)

            def gather(ix, iy):
                idx = (ix * Wp + iy).astype(jnp.int32).reshape(B, 1, -1)
                return jnp.take_along_axis(xf, idx, axis=2).reshape(B, C, H, W, N)
            g_lt = ((1 + (x0 - px)) * (1 + (y0 - py)))[:, None]
            g_rb = ((1 - (x1 - px)) * (1 - (y1 - py)))[:, None]
            g_lb = ((1 + (x0 - px)) * (1 - (y1 - py)))[:, None]
            g_rt = ((1 - (x1 - px)) * (1 + (y0 - py)))[:, None]
            xo = g_lt * gather(x0, y0) + g_rb * gather(x1, y1) + g_lb * gather(x0, y1) + g_rt * gather(x1, y0)
            xo = xo.reshape(B, C, H, W, 3, 3).transpose(0, 1, 2, 4, 3, 5).reshape(B, C, H * 3, W * 3)
            return jax.lax.conv_general_dilated(xo, w, (3, 3), 'VALID', dimension_numbers=('NCHW', 'OIHW', 'NCHW'))
        out = jax.nn.relu(batchnorm(conv2d(x, w1), g1, b1))
        offsets = conv2d(out, w_off) + b_off[None, :, None, None]
        out = batchnorm(deform_conv(out, offsets, w2), g2, b2)
        return jax.nn.relu(out + x)

    def _gn(v, G=32, eps=1e-5):
        B_, C_, H_, W_ = v.shape
        g = v.reshape(B_, G, C_ // G, H_, W_)
        m = jnp.mean(g, axis=(2, 3, 4), keepdims=True)
        s = jnp.var(g, axis=(2, 3, 4), keepdims=True)
        return ((g - m) / jnp.sqrt(s + eps)).reshape(v.shape)

    def _ln_c(v, eps=1e-6):
        m = jnp.mean(v, axis=1, keepdims=True)
        s = jnp.var(v, axis=1, keepdims=True)
        return (v - m) / jnp.sqrt(s + eps)

    def _ln_t(v, eps=1e-5):
        m = jnp.mean(v, axis=-1, keepdims=True)
        s = jnp.var(v, axis=-1, keepdims=True)
        return (v - m) / jnp.sqrt(s + eps)

    def _to_tokens(v):
        B_, C_, H_, W_ = v.shape
        return v.reshape(B_, C_, H_ * W_).transpose(0, 2, 1)
    def _from_tokens(t, like):
        B_, C_, H_, W_ = like.shape
        return t.transpose(0, 2, 1).reshape(B_, C_, H_, W_)

    x = _L0_conv_ref(x, L0_conv_norm_w, L0_conv_norm_b, L0_conv_qkv_w, L0_conv_qkv_b, L0_conv_proj_w, L0_conv_proj_b)
    x = _L1_conv_ref(x, L1_conv_w1, L1_conv_g1, L1_conv_b1, L1_conv_w_off, L1_conv_b_off, L1_conv_w2, L1_conv_g2, L1_conv_b2)
    return x


_drawn_inputs = setup_inputs


def setup_inputs(seed=0):
    import zlib

    import numpy as np

    out = dict(_drawn_inputs(seed))
    spreads = {'L0_conv_norm_w': (1.0, 0.2),
     'L0_conv_norm_b': (0.0, 0.1),
     'L0_conv_qkv_b': (0.0, 0.1),
     'L0_conv_proj_b': (0.0, 0.1),
     'L1_conv_g1': (1.0, 0.2),
     'L1_conv_b1': (0.0, 0.1),
     'L1_conv_b_off': (0.0, 0.1),
     'L1_conv_g2': (1.0, 0.2),
     'L1_conv_b2': (0.0, 0.1)}
    factors = {}
    for name, (base, spread) in spreads.items():
        noise = np.random.default_rng([zlib.crc32(name.encode()), seed]).standard_normal(out[name].shape)
        drawn = base * np.exp(spread * noise) if base else spread * noise
        out[name] = jnp.asarray(drawn.astype(out[name].dtype))
    for name, factor in factors.items():
        out[name] = (out[name] * factor).astype(out[name].dtype)
    return out
```

```python
import concourse.bass as bass
from concourse import mybir
from contextlib import ExitStack

F32 = mybir.dt.float32
F16 = mybir.dt.float16
I32 = mybir.dt.int32
ALU = mybir.AluOpType
ACT = mybir.ActivationFunctionType
AX = mybir.AxisListType

B, C, HH, WW = 4, 128, 64, 64
N = HH * WW
NG_SIZE = C // 32
EPS = 1e-5
NCH = N // 512
SBQ = 256
NSB = N // SBQ
UPS = 8
GPS = N // 256
LAG = 3
PSCALE = 2.0 ** 14
TAPS = 9
NOFF = 2 * TAPS
WIN = 6
BLOCKS = WIN // 2
UNITS = 3 * BLOCKS
REACH = float(WIN // 2 - 1)
SHIFTS = (HH + WIN - 1) // WIN
GAP = WIN * (SHIFTS + 1)
HALF_TILES = 16
XT_WINDOWS = 2 * HALF_TILES + WIN - 1
ROWS = 2 * WIN * SHIFTS + (B - 1) * (HH + GAP) + GAP + 32 + XT_WINDOWS
TOP = WIN // 2
OPEN = 32

W_QKV, W_PROJ = 0, 3 * C
W_1 = W_PROJ + C
W_2 = W_1 + TAPS * C
W_OFF = W_2 + TAPS * C
W_MM = W_OFF + TAPS * NOFF
V_NW, V_NB, V_BQ, V_BK, V_BV, V_BP, V_G1, V_B1, V_G2, V_B2 = range(W_MM, W_MM + 10)
W_BOFF = W_MM + 10
W_ALL = W_BOFF + NOFF

K_ID, K_GRP, K_ONE, K_YC = 0, 128, 256, 384
K_JH = K_YC + TAPS
K_YI = K_JH + WIN
K_ALL = K_YI + WW

GN_STEPS = 9
L1_VAR1, L1_AB1, L1_MAX, L1_GT, L1_FLAG, L1_VAR2, L1_AB2 = 2, 5, 9, 11, 14, 16, 19


def build(nc, x, weights, consts, out):
    x1_dram = nc.dram_tensor("x1_scratch", [B, C, N], F32, kind="Internal").ap()
    xt_dram = nc.dram_tensor("xt_scratch", [ROWS * WW, 2 * C], F16, kind="Internal").ap()
    out = out.rearrange("b c h w -> b c (h w)")
    x = x.rearrange("b c h w -> b c (h w)")

    ctx = ExitStack()
    with ctx:
        def sem(name):
            return ctx.enter_context(nc.semaphore(name))

        def sb_in(scope, name, shape, dt):
            return scope.enter_context(nc.sbuf_tensor(name, shape, dt))

        WF = sb_in(ctx, "weights_f32", [128, W_ALL], F32)
        WH = sb_in(ctx, "weights_hi", [128, W_MM], F16)
        WL = sb_in(ctx, "weights_lo", [128, W_MM], F16)
        CN = sb_in(ctx, "constants", [128, K_ALL], F32)
        OW1 = sb_in(ctx, "offset_w_hi_lo", [128, TAPS, 2 * NOFF], F16)
        OW2 = sb_in(ctx, "offset_w_hi_zero", [128, TAPS, 2 * NOFF], F16)
        SM = sb_in(ctx, "small", [128, 64], F32)
        ZT = sb_in(ctx, "zeros_f16", [128, 768], F16)
        CNT = sb_in(ctx, "pass_counts", [1, 2], I32)
        ident = CN[:, K_ID:K_ID + 128]

        l0 = ExitStack()
        XIN = sb_in(l0, "x_image", [128, N], F32)
        HNh = sb_in(l0, "h_hi", [128, N], F16)
        HNl = sb_in(l0, "h_lo", [128, N], F16)
        Qh = sb_in(l0, "q_hi", [128, N], F16)
        Ql = sb_in(l0, "q_lo", [128, N], F16)
        Kh = sb_in(l0, "k_hi", [128, N], F16)
        Kl = sb_in(l0, "k_lo", [128, N], F16)
        Vh = sb_in(l0, "vT_hi", [128, N], F16)
        Vl = sb_in(l0, "vT_lo", [128, N], F16)
        P = sb_in(l0, "probs", [128, 2, 2, N], F32)
        PTh = sb_in(l0, "probsT_hi", [128, 4, 512], F16)
        PTl = sb_in(l0, "probsT_lo", [128, 4, 512], F16)
        Oh = sb_in(l0, "attn_hi", [128, 2, SBQ], F16)
        Ol = sb_in(l0, "attn_lo", [128, 2, SBQ], F16)
        XR = sb_in(l0, "x_residual", [128, 2, SBQ], F32)
        XO = sb_in(l0, "x1_out", [128, 2, SBQ], F32)
        NM = sb_in(l0, "neg_max", [128, 2, 2, 4], F32)
        NMF = sb_in(l0, "neg_max_row", [128, 2, 2, 1], F32)
        LS = sb_in(l0, "chunk_sums", [128, 2, 2, 4], F32)
        AL = sb_in(l0, "chunk_rescale", [128, 2, 2, 4], F32)
        BE = sb_in(l0, "chunk_factor", [128, 2, 2, 4], F32)
        TS = sb_in(l0, "sum_scratch", [128, 2, 2, 6], F32)
        GATE = sb_in(l0, "pool_gate", [128, 4], F32)
        ST6 = sb_in(l0, "gn_stats", [128, NCH, 6], F32)
        l0.close()

        l1 = ExitStack()
        Y = sb_in(l1, "y1_then_z", [128, B, N], F32)
        OFF = sb_in(l1, "offsets", [128, B * 32, NOFF], F32)
        PY = sb_in(l1, "sample_cols", [128, B * 32, TAPS], F32)
        BS = sb_in(l1, "bn_stats", [128, B * NCH, 6], F32)
        XS = sb_in(l1, "xt_stage", [128, 2, 4, 2 * C], F16)
        l1a = ExitStack()
        XC = sb_in(l1a, "x1_rows", [128, 4, 512], F32)
        PDh = sb_in(l1a, "padded_hi", [128, HH + 2, WW + 2], F16)
        PDl = sb_in(l1a, "padded_lo", [128, HH + 2, WW + 2], F16)
        HT = sb_in(l1a, "h1_rows", [128, 2, 512], F32)
        OE = sb_in(l1a, "offset_rows", [128, 2, 512], F32)
        OR = sb_in(l1a, "offset_parts", [128, B * 32, 2 * NOFF], F32)
        l1a.close()
        l1b = ExitStack()
        XT = sb_in(l1b, "xt_windows", [128, 2, 2, (XT_WINDOWS + 1) // 2, 2 * C], F16)
        HX = sb_in(l1b, "row_hats", [128, 2, HALF_TILES * TAPS, WIN], F32)
        DD = sb_in(l1b, "col_distance", [128, 2, TAPS, WW], F32)
        HY = sb_in(l1b, "col_hats", [128, 2, TAPS, WW], F32)
        SS = sb_in(l1b, "interp", [128, 2, TAPS, WIN, WW], F32)
        STh = sb_in(l1b, "interpT_hi", [128, 3, 384], F16)
        STl = sb_in(l1b, "interpT_lo", [128, 3, 384], F16)
        SOh = sb_in(l1b, "sampled_hi", [128, 3, 384], F16)
        SOl = sb_in(l1b, "sampled_lo", [128, 3, 384], F16)
        l1b.close()
        l1c = ExitStack()
        FX = sb_in(l1c, "final_x1", [128, 4, 1024], F32)
        FO = sb_in(l1c, "final_out", [128, 4, 1024], F32)
        l1c.close()
        l1.close()

        PS = ctx.enter_context(nc.psum_tensor("psum", [128, 8, 512], F32))

        s_w = sem("weights_loaded")
        s_k = sem("constants_loaded")
        s_zf = sem("zero_rows_stored")
        s_open = sem("opened")
        s_set = sem("setup_steps")
        s_wh = sem("weights_hi_ready")
        s_ws = sem("weights_ready")
        s_bp = sem("bias_product")
        s_pz = sem("pool_cleared")
        s_x = sem("image_loaded")
        s_xr = [sem(f"residual_loaded{i}") for i in range(2)]
        s_xo = [sem(f"x1_stored{i}") for i in range(2)]
        s_xc = [sem(f"rows_loaded{i}") for i in range(4)]
        s_xs = [sem(f"xt_stored{i}") for i in range(2)]
        s_ld = [sem(f"windows_loaded{i}") for i in range(2)]
        s_fx = [sem(f"final_loaded{i}") for i in range(4)]
        s_fo = [sem(f"final_stored{i}") for i in range(4)]

        names = dict(
            gn="gn_steps", gp="gn_product", rs="gn_rstd", h32="h_affine", hh="h_hi_ready", hl="h_lo_ready",
            qkv="qkv_product", evh="qkv_hi_ready", evl="qkv_lo_ready",
            S="scores", mx="chunk_max", exp="chunk_exp", nm="row_max", al="rescale", bc="sum_steps",
            be="factor", pp="probs_scaled", T="probs_transposed", hi="probsT_hi_ready", lo="probsT_lo_ready",
            av="values", oh="attn_hi_ready", ol="attn_lo_ready", pj="projected", x1="x1_ready",
            chi="rows_hi_ready", clo="rows_lo_ready", cv="conv1", ye="y1_ready", bs="y1_stats",
            hA="h1_ready", hp="h1_split", of="offset_conv", oe="offset_rows_ready", ot="offset_transposed",
            oc="offset_copied", xt="h1_transposed", xth="h1T_hi_ready", xe="h1T_ready",
            hd="row_distance", hb="row_abs", hx="row_hats_ready", pq="interp_part_ready", dd="distance_ready", ab="distance_abs", hy="col_hat_ready", pr="interp_ready",
            tt="interp_transposed", th="interpT_hi_ready", tl="interpT_lo_ready", mm="sampled",
            xh="sampled_hi_ready", xl="sampled_lo_ready", c2="conv2", z="z_added", dsh="shift_steps",
            l1="bn_steps", l1p="bn_rstd", fl="flag_product", fz="z_cleared", fr="final_sum", fa="final_relu")
        s = {k: sem(v) for k, v in names.items()}

        def after(eng, key, count):
            eng.wait_ge(s[key], count + OPEN)

        def stored(eng, slot_sem, n):
            eng.wait_ge(slot_sem, n * 16 + OPEN)

        def vec(i):
            return WF[:, i:i + 1]

        block = ctx.enter_context(nc.Block())

        def product(eng, key, hid, q, tl, half, par, dx):
            after(eng, "hx", hid + 1)
            after(eng, "hy", q + 1)
            after(eng, "tt", (q - 1) * UNITS)
            hy = HY[:, par, 3 * dx:3 * dx + 3, None, :].to_broadcast([128, 3, WIN, WW])
            hx = HX[:, half, bass.ds(tl * TAPS + 3 * dx, 3), :].rearrange("p k j -> p (k j)")
            eng.tensor_tensor(SS[:, par, 3 * dx:3 * dx + 3, :, :], hy, hx[:, :, None].to_broadcast([128, 3 * WIN, WW]),
                              ALU.mult).then_inc(s[key], 1)

        @block.sync
        def _(sp):
            sp.dma_start(WF[:, :], weights).then_inc(s_w, 16)
            sp.dma_start(CN[:, :], consts).then_inc(s_k, 16)
            sp.dma_start(XIN[:, :], x[0]).then_inc(s_x, 16)
            sp.wait_ge(s_open, 1)
            sp.wait_ge(s_pz, 1)
            for i in range(B + 1):
                r0 = i * (HH + GAP)
                dst = xt_dram[r0 * WW:(r0 + GAP) * WW, :].rearrange("(p a b) c -> p a (b c)", p=128, b=3)
                sp.dma_start(dst, ZT[:, None, :].to_broadcast([128, GAP * WW // 384, 768])).then_inc(s_zf, 16)

            def superblocks(b):
                with sp.Fori(0, NSB // 2) as t:
                    for par in range(2):
                        after(sp, "x1", b * NSB + t * 2 + (par - 1))
                        sp.dma_start(XR[:, par, :], x[b, :, bass.ds(t * (2 * SBQ) + par * SBQ, SBQ)]).then_inc(s_xr[par], 16)
                    for par in range(2):
                        after(sp, "x1", b * NSB + t * 2 + (par + 1))
                        sp.dma_start(x1_dram[b, :, bass.ds(t * (2 * SBQ) + par * SBQ, SBQ)], XO[:, par, :]).then_inc(s_xo[par], 16)

            with sp.Fori(0, B - 1) as b:
                after(sp, "hl", (b + 1) * NCH)
                sp.dma_start(XIN[:, :], x[b + 1]).then_inc(s_x, 16)
                superblocks(b)
            superblocks(B - 1)

            for par in range(2):
                stored(sp, s_xo[par], B * NSB // 2)
            with sp.Fori(0, B) as b:
                for rb in range(NCH):
                    after(sp, "clo", b * NCH + (rb - 3))
                    sp.dma_start(XC[:, rb % 4, :], x1_dram[b, :, 512 * rb:512 * rb + 512]).then_inc(s_xc[rb % 4], 16)
            with sp.Fori(0, B) as b:
                for rb in range(NCH):
                    after(sp, "xe", b * NCH + (rb + 1))
                    row = b * (HH + GAP) + (GAP + 8 * rb)
                    sp.dma_start(xt_dram[bass.ds(row * WW, 8 * WW), :].rearrange("(t p) c -> p t c", p=128),
                                 XS[:, rb % 2, :, :]).then_inc(s_xs[rb % 2], 16)
            for i in range(2):
                stored(sp, s_xs[i], B * NCH // 2)
            sp.wait_ge(s_zf, 16 * (B + 1))
            after(sp, "l1", L1_FLAG)
            npass = sp.value_load(CNT[0:1, 0:1], min_val=1, max_val=2 * SHIFTS + 1)
            first = sp.value_load(CNT[0:1, 1:2], min_val=0, max_val=SHIFTS)
            with sp.Fori(0, npass) as n:
                with sp.Fori(0, B) as b:
                    for half in range(2):
                        row = (n + first) * WIN + b * (HH + GAP) + (GAP - TOP + 32 * half - WIN * SHIFTS)
                        after(sp, "z", n * 128 + b * 32 + (half - 1) * HALF_TILES)
                        for odd in range(2):
                            for w0, w1 in ((0, 10), (10, XT_WINDOWS // 2 + 1 - odd)):
                                src = xt_dram[bass.ds((row + (odd + 2 * w0)) * WW, (w1 - w0) * 128), :]
                                sp.dma_start(XT[:, half, odd, w0:w1, :],
                                             src.rearrange("(w p) c -> p w c", p=128)).then_inc(s_ld[half], 16)
            after(sp, "l1", L1_VAR2)
            with sp.Fori(0, B) as b:
                for i in range(4):
                    after(sp, "fr", b * 4 + (i - 3))
                    sp.dma_start(FX[:, i, :], x1_dram[b, :, 1024 * i:1024 * i + 1024]).then_inc(s_fx[i], 16)
                for i in range(4):
                    after(sp, "fa", b * 4 + (i + 1))
                    sp.dma_start(out[b, :, 1024 * i:1024 * i + 1024], FO[:, i, :]).then_inc(s_fo[i], 16)
            for i in range(4):
                stored(sp, s_fo[i], B)

        @block.gpsimd
        def _(po):
            for k in s:
                po.sem_inc(s[k], OPEN)
            for k in s_xo + s_xs + s_fo:
                po.sem_inc(k, OPEN)
            po.sem_inc(s_open, 1)
            po.memset(ZT[:, :], 0.0).then_inc(s_pz, 1)
            po.memset(OW2[:, :, :], 0.0).then_inc(s_pz, 1)
            po.memset(SM[:, 0:1], -0.5).then_inc(s_pz, 1)
            po.memset(SM[:, 1:2], 1.0).then_inc(s_pz, 1)
            po.wait_ge(s_pz, 4)
            with po.Fori(0, B) as b:
                after(po, "gn", b * GN_STEPS + 6)
                po.tensor_tensor(SM[:, 8:9], SM[:, 7:8], SM[:, 0:1], ALU.pow).then_inc(s["rs"], 1)
                with po.Fori(0, NSB // 2) as t:
                    for par in range(2):
                        for i in range(2):
                            v = b * (2 * NSB) + t * 4 + (2 * par + i)
                            after(po, "pp", v * 4)
                            after(po, "be", v + 1)
                            po.tensor_tensor(GATE[:, 0:4], BE[:, par, i, :], BE[:, par, i, :], ALU.mult)
                            for j in range(4):
                                pj = P[:, par, i, 1024 * j:1024 * j + 1024]
                                po.tensor_scalar(pj, pj, BE[:, par, i, j:j + 1], PSCALE, ALU.mult, ALU.mult).then_inc(s["pp"], 1)
            after(po, "x1", B * NSB)
            after(po, "pj", B * NSB)
            po.memset(OE[:, :, :], 0.0)
            for t in (PDh, PDl):
                po.memset(t[:, 0, :], 0.0)
                po.memset(t[:, HH + 1, :], 0.0)
                po.memset(t[:, 1:HH + 1, 0:1], 0.0)
                po.memset(t[:, 1:HH + 1, WW + 1:WW + 2], 0.0).then_inc(s_pz, 1)
            after(po, "l1", L1_VAR1)
            po.tensor_tensor(SM[:, 12:13], SM[:, 11:12], SM[:, 0:1], ALU.pow).then_inc(s["l1p"], 1)
            after(po, "hA", B * NCH)
            for b in range(B):
                po.memset(Y[:, b, :], 0.0).then_inc(s["fz"], 1)
            after(po, "l1", L1_FLAG)
            npass = po.value_load(CNT[0:1, 0:1], min_val=1, max_val=2 * SHIFTS + 1)

            def distance(q, tile, par):
                after(po, "hy", q - 1)
                py = PY[:, bass.ds(tile, 1), :].rearrange("p a k -> p (a k)")
                po.tensor_tensor(DD[:, par, :, :], CN[:, K_YI:K_YI + WW][:, None, :].to_broadcast([128, TAPS, WW]),
                                 py[:, :, None].to_broadcast([128, TAPS, WW]), ALU.subtract).then_inc(s["dd"], 1)

            with po.Fori(0, npass) as n:
                with po.Fori(0, B) as b:
                    for half in range(2):
                        hid, t0 = n * (2 * B) + b * 2 + half, b * 32 + half * HALF_TILES
                        q0 = n * 128 + t0
                        after(po, "pr", q0 * 2)
                        po.tensor_tensor(HX[:, half, :, :].rearrange("p (t k) j -> p t k j", k=TAPS),
                                         CN[:, K_JH:K_JH + WIN][:, None, None, :].to_broadcast([128, HALF_TILES, TAPS, WIN]),
                                         OFF[:, bass.ds(t0, HALF_TILES), 0:TAPS][:, :, :, None].to_broadcast([128, HALF_TILES, TAPS, WIN]),
                                         ALU.subtract).then_inc(s["hd"], 1)
                        distance(q0, t0, 0)
                        distance(q0 + 1, t0 + 1, 1)
                        with po.Fori(0, HALF_TILES // 2 - 1) as u:
                            for par in range(2):
                                tl = u * 2 + par
                                product(po, "pq", hid, q0 + tl, tl, half, par, 2)
                                distance(q0 + (tl + 2), t0 + (tl + 2), par)
                        for par in range(2):
                            tl = HALF_TILES - 2 + par
                            product(po, "pq", hid, q0 + tl, tl, half, par, 2)
            after(po, "l1", L1_VAR2)
            po.tensor_tensor(SM[:, 22:23], SM[:, 21:22], SM[:, 0:1], ALU.pow).then_inc(s["l1p"], 1)

        @block.scalar
        def _(act):
            act.wait_ge(s_open, 1)
            act.wait_ge(s_set, 1)
            act.activation(WH[:, :], WF[:, 0:W_MM], ACT.Copy).then_inc(s_wh, 1)

            def unit(b, sb, par, k, older, scores, late, values):
                if late:
                    par_, sb_ = (par, sb) if k else (1 - par, sb - 1)
                    i, j = divmod((k - 1) % UPS, 4)
                    U = b * (NSB * UPS) + sb * UPS + (k - 1)
                    after(act, "mx", U + 1)
                    after(act, "T", b * (NSB * GPS) + sb_ * GPS + (4 * j + 4 - 2 * GPS))
                    sc = PS[:, 2 * (j % 2):2 * (j % 2) + 2, :].rearrange("p a n -> p (a n)")
                    act.activation(P[:, par_, i, 1024 * j:1024 * j + 1024], sc, ACT.Exp, bias=NM[:, par_, i, j:j + 1],
                                   accum_out=LS[:, par_, i, j:j + 1]).then_inc(s["exp"], 1)
                    if j == 3:
                        V = b * (2 * NSB) + sb_ * 2 + i
                        after(act, "nm", V + 1)
                        act.activation(AL[:, par_, i, :], NM[:, par_, i, :], ACT.Exp, scale=-1.0,
                                       bias=NMF[:, par_, i, :]).then_inc(s["al"], 1)
                if values is not None:
                    back, g0 = values
                    for g in (g0, g0 + 1):
                        G = b * (NSB * GPS) + (sb - back) * GPS + g
                        after(act, "T", G + 1)
                        after(act, "av", G - 3)
                        act.activation(PTh[:, g % 4, :], PS[:, 4 + g % 2, :], ACT.Copy).then_inc(s["hi"], 1)
                    if g0 == 2 and older is not None:
                        attn_out(b, sb - 2, par)

            def attn_out(b, sb, par):
                after(act, "av", b * (NSB * GPS) + sb * GPS + GPS)
                act.activation(Oh[:, par, :], PS[:, 6 + par, 0:SBQ], ACT.Copy, scale=1.0 / PSCALE).then_inc(s["oh"], 1)

            with act.Fori(0, B) as b:
                after(act, "qkv", b * 3 * NCH)
                for c in range(NCH):
                    after(act, "h32", b * NCH + (c + 1))
                    act.activation(HNh[:, 512 * c:512 * c + 512], XIN[:, 512 * c:512 * c + 512], ACT.Copy).then_inc(s["hh"], 1)
                after(act, "av", b * NSB * GPS)
                for u in range(3 * NCH):
                    c, kind = divmod(u, 3)
                    after(act, "qkv", b * (3 * NCH) + (u + 1))
                    dst = (Qh, Kh, Vh)[kind][:, 512 * c:512 * c + 512]
                    if kind == 2:
                        act.activation(dst, PS[:, u % 8, :], ACT.Copy).then_inc(s["evh"], 1)
                    else:
                        bias = SM[:, 2:3] if kind == 0 else vec(V_BK)
                        act.activation(dst, PS[:, u % 8, :], ACT.Identity, bias=bias).then_inc(s["evh"], 1)
                schedule(act, b, unit)
                attn_out(b, NSB - 1, (NSB - 1) % 2)

            after(act, "x1", B * NSB)
            after(act, "pj", B * NSB)
            act.wait_ge(s_pz, 6)
            with act.Fori(0, B) as b:
                for rb in range(NCH + 1):
                    if rb < NCH:
                        act.wait_ge(s_xc[rb % 4], (b * 2 + (rb // 4 + 1)) * 16)
                        after(act, "cv", b * NCH + (min(rb + 2, NCH) - NCH))
                        act.activation(PDh[:, 1 + 8 * rb:9 + 8 * rb, 1:WW + 1],
                                       XC[:, rb % 4, :].rearrange("p (r w) -> p r w", w=WW), ACT.Copy).then_inc(s["chi"], 1)
                    if rb:
                        after(act, "cv", b * NCH + rb)
                        yd = Y[:, bass.ds(b, 1), 512 * rb - 512:512 * rb].rearrange("p a n -> p (a n)")
                        act.activation(yd, PS[:, (rb - 1) % 4, :], ACT.Copy).then_inc(s["ye"], 1)
            after(act, "l1", L1_AB1)
            after(act, "ye", B * NCH)
            with act.Fori(0, B) as b:
                for rb in range(NCH + 3):
                    if rb < NCH:
                        after(act, "hp", b * NCH + (rb - 1))
                        after(act, "xt", b * NCH + (rb - 1))
                        ys = Y[:, bass.ds(b, 1), 512 * rb:512 * rb + 512].rearrange("p a n -> p (a n)")
                        act.activation(HT[:, rb % 2, :], ys, ACT.Relu, scale=SM[:, 13:14], bias=SM[:, 15:16]).then_inc(s["hA"], 1)
                    if 1 <= rb < NCH + 1:
                        after(act, "xt", b * NCH + rb)
                        stored(act, s_xs[(rb - 1) % 2], b * (NCH // 2) + (rb - 1) // 2)
                        src = PS[:, 4 + (rb - 1) % 2, :].rearrange("p (t c) -> p t c", c=C)
                        act.activation(XS[:, (rb - 1) % 2, :, 0:C], src, ACT.Copy).then_inc(s["xth"], 1)
                    if 2 <= rb < NCH + 2:
                        m = b * NCH + (rb - 2)
                        after(act, "of", m + 1)
                        after(act, "ot", m - 1)
                        act.activation(OE[0:2 * NOFF, rb % 2, :], PS[0:2 * NOFF, rb % 2, :], ACT.Copy).then_inc(s["oe"], 1)
                    if rb >= 3:
                        after(act, "ot", b * NCH + (rb - 2))
                        src = PS[:, 2 + (rb - 3) % 2, :].rearrange("p (t k) -> p t k", t=4)[:, :, 0:2 * NOFF]
                        act.activation(OR[:, bass.ds(b * 32 + 4 * (rb - 3), 4), :], src, ACT.Copy).then_inc(s["oc"], 1)
            after(act, "l1", L1_FLAG)
            after(act, "xe", B * NCH)
            npass = act.value_load(CNT[0:1, 0:1], min_val=1, max_val=2 * SHIFTS + 1)

            def sampled(q, dx):
                after(act, "mm", q * UNITS + (BLOCKS * dx + BLOCKS))
                after(act, "c2", q * 3 + (dx - 2))
                act.activation(SOh[:, dx, :], PS[:, 3 + dx, 0:384], ACT.Copy).then_inc(s["xh"], 1)

            def col_abs(q, par):
                after(act, "dd", q + 1)
                act.activation(DD[:, par, :, :], DD[:, par, :, :], ACT.Abs).then_inc(s["ab"], 1)

            def col_hat(q, par):
                after(act, "ab", q + 1)
                after(act, "pr", q * 2 - 2)
                after(act, "pq", q - 1)
                act.activation(HY[:, par, :, :], DD[:, par, :, :], ACT.Relu, scale=-1.0, bias=1.0).then_inc(s["hy"], 1)

            def tile(q, tl, par, cur, prev, nxt):
                for v in range(UNITS):
                    if cur:
                        after(act, "tt", q * UNITS + (v + 1))
                        after(act, "mm", q * UNITS + (v - 2))
                        act.activation(STh[:, v % 3, :], PS[:, v % 3, 0:384], ACT.Copy).then_inc(s["th"], 1)
                    if nxt and v == 0:
                        col_abs(q + 1, 1 - par)
                    if nxt and v == 1:
                        col_hat(q + 1, 1 - par)
                    if prev and v == 2:
                        sampled(q - 1, 2)
                    if cur and v in (5, 8):
                        sampled(q, v // 3 - 1)

            with act.Fori(0, npass) as n:
                with act.Fori(0, B) as b:
                    for half in range(2):
                        hid = n * (2 * B) + b * 2 + half
                        q0 = n * 128 + b * 32 + half * HALF_TILES
                        hx = HX[:, half, :, :]
                        after(act, "dsh", n + B * NCH)
                        after(act, "hd", hid + 1)
                        act.activation(hx, hx, ACT.Abs, bias=SM[:, 31:32]).then_inc(s["hb"], 1)
                        after(act, "hb", hid + 1)
                        act.activation(hx, hx, ACT.Relu, scale=-1.0, bias=1.0).then_inc(s["hx"], 1)
                        col_abs(q0, 0)
                        col_hat(q0, 0)
                        half_image(act, q0, tile)
            after(act, "l1", L1_AB2)
            with act.Fori(0, B) as b:
                for i in range(4):
                    after(act, "fr", b * 4 + (i + 1))
                    stored(act, s_fo[i], b)
                    act.activation(FO[:, i, :], FX[:, i, :], ACT.Relu, bias=SM[:, 25:26]).then_inc(s["fa"], 1)

        @block.vector
        def _(ve):
            step = [0]

            def link(ins):
                step[0] += 1
                ins.then_inc(s_set, 1)
                ve.wait_ge(s_set, step[0])

            ve.wait_ge(s_open, 1)
            ve.wait_ge(s_w, 16)
            link(ve.tensor_scalar(WF[:, 0:C], WF[:, 0:C], float(C) ** -0.5, None, ALU.mult))
            link(ve.tensor_scalar(SM[:, 2:3], vec(V_BQ), float(C) ** -0.5, None, ALU.mult))
            ve.wait_ge(s_wh, 1)
            link(ve.tensor_tensor(WL[:, :], WF[:, 0:W_MM], WH[:, :], ALU.subtract))
            ve.wait_ge(s_pz, 4)
            oh = WH[:, W_OFF:W_MM].rearrange("p (k o) -> p k o", k=TAPS)
            ol = WL[:, W_OFF:W_MM].rearrange("p (k o) -> p k o", k=TAPS)
            link(ve.tensor_copy(OW1[:, :, 0:NOFF], oh))
            link(ve.tensor_copy(OW1[:, :, NOFF:2 * NOFF], ol))
            link(ve.tensor_copy(OW2[:, :, 0:NOFF], oh))
            ve.wait_ge(s_bp, 1)
            ve.tensor_tensor(SM[:, 3:4], PS[:, 7, 0:1], vec(V_BP), ALU.add).then_inc(s_ws, 1)
            ve.wait_ge(s_ws, 1)

            def beta(b, sb, par, i):
                V = b * (2 * NSB) + sb * 2 + i
                after(ve, "al", V + 1)
                t = TS[:, par, i, :]
                ve.tensor_tensor(t[:, 0:4], AL[:, par, i, :], LS[:, par, i, :], ALU.mult).then_inc(s["bc"], 1)
                after(ve, "bc", V * 3 + 1)
                ve.reduce_sum(t[:, 4:5], t[:, 0:4], AX.X).then_inc(s["bc"], 1)
                after(ve, "bc", V * 3 + 2)
                ve.reciprocal(t[:, 5:6], t[:, 4:5]).then_inc(s["bc"], 1)
                after(ve, "bc", V * 3 + 3)
                ve.tensor_scalar(BE[:, par, i, :], AL[:, par, i, :], t[:, 5:6], None, ALU.mult).then_inc(s["be"], 1)

            def attn_out(b, sb, par):
                after(ve, "oh", b * NSB + sb + 1)
                ve.scalar_tensor_tensor(Ol[:, par, :], PS[:, 6 + par, 0:SBQ], 1.0 / PSCALE, Oh[:, par, :],
                                        ALU.mult, ALU.subtract).then_inc(s["ol"], 1)

            def x1_out(b, sb, half_sb, par):
                after(ve, "pj", b * NSB + sb + 1)
                ve.wait_ge(s_xr[par], (b * (NSB // 2) + half_sb + 1) * 16)
                stored(ve, s_xo[par], b * (NSB // 2) + half_sb)
                ve.scalar_tensor_tensor(XO[:, par, :], PS[:, 6 + par, SBQ:2 * SBQ], SM[:, 3:4], XR[:, par, :],
                                        ALU.add, ALU.add).then_inc(s["x1"], 1)

            def unit(b, sb, par, k, older, scores, late, values):
                if scores:
                    i, j = divmod(k, 4)
                    U = b * (NSB * UPS) + sb * UPS + k
                    after(ve, "S", U + 1)
                    sc = PS[:, 2 * (k % 2):2 * (k % 2) + 2, :].rearrange("p a n -> p (a n)")
                    ve.tensor_reduce(NM[:, par, i, j:j + 1], sc, AX.X, ALU.max, negate=True).then_inc(s["mx"], 1)
                    if j == 3:
                        after(ve, "mx", U + 1)
                        ve.tensor_reduce(NMF[:, par, i, :], NM[:, par, i, :], AX.X, ALU.min).then_inc(s["nm"], 1)
                if values is not None:
                    back, g0 = values
                    for g in (g0, g0 + 1):
                        G = b * (NSB * GPS) + (sb - back) * GPS + g
                        after(ve, "hi", G + 1)
                        ve.tensor_tensor(PTl[:, g % 4, :], PS[:, 4 + g % 2, :], PTh[:, g % 4, :], ALU.subtract).then_inc(s["lo"], 1)
                        if g == g0:
                            row_factors(b, sb, par, k, late)
                    if g0 == 2 and older is not None:
                        attn_out(b, sb - 2, par)
                    if g0 == 8 and older is not None:
                        x1_out(b, sb - 2, older, par)
                else:
                    row_factors(b, sb, par, k, late)

            def row_factors(b, sb, par, k, late):
                if late and k == 4:
                    beta(b, sb, par, 0)
                elif late and k == 0:
                    beta(b, sb - 1, 1 - par, 1)

            with ve.Fori(0, B) as b:
                ve.wait_ge(s_x, b * 16 + 16)
                g0 = b * GN_STEPS
                for c in range(NCH):
                    ins = ve.bn_stats(ST6[:, c, :], XIN[:, 512 * c:512 * c + 512])
                ins.then_inc(s["gn"], 1)
                after(ve, "gn", g0 + 1)
                ve.tensor_copy(SM[:, 40:41], ST6[:, NCH - 1, 1:2])
                ve.bn_aggr(SM[:, 4:6], ST6[:, :, :].rearrange("p a b -> p (a b)")).then_inc(s["gn"], 1)
                after(ve, "gn", g0 + 2)
                ve.scalar_tensor_tensor(SM[:, 5:6], SM[:, 4:5], SM[:, 4:5], SM[:, 5:6], ALU.mult, ALU.add).then_inc(s["gn"], 1)
                after(ve, "gp", b + 1)
                ve.tensor_copy(SM[:, 9:11], PS[:, 7, 0:2]).then_inc(s["gn"], 1)
                after(ve, "gn", g0 + 4)
                ve.scalar_tensor_tensor(SM[:, 6:7], SM[:, 9:10], SM[:, 9:10], SM[:, 10:11], ALU.mult, ALU.subtract).then_inc(s["gn"], 1)
                after(ve, "gn", g0 + 5)
                ve.tensor_scalar(SM[:, 7:8], SM[:, 6:7], -1.0, EPS, ALU.mult, ALU.add).then_inc(s["gn"], 1)
                after(ve, "rs", b + 1)
                ve.tensor_tensor(SM[:, 16:17], SM[:, 8:9], vec(V_NW), ALU.mult).then_inc(s["gn"], 1)
                after(ve, "gn", g0 + 7)
                ve.tensor_tensor(SM[:, 17:18], SM[:, 9:10], SM[:, 16:17], ALU.mult).then_inc(s["gn"], 1)
                after(ve, "gn", g0 + 8)
                ve.tensor_tensor(SM[:, 18:19], vec(V_NB), SM[:, 17:18], ALU.subtract).then_inc(s["gn"], 1)
                after(ve, "gn", g0 + 9)
                for c in range(NCH + 1):
                    if c < NCH:
                        xc = XIN[:, 512 * c:512 * c + 512]
                        ve.tensor_scalar(xc, xc, SM[:, 16:17], SM[:, 18:19], ALU.mult, ALU.add).then_inc(s["h32"], 1)
                    if c:
                        after(ve, "hh", b * NCH + c)
                        sl = slice(512 * c - 512, 512 * c)
                        ve.tensor_tensor(HNl[:, sl], XIN[:, sl], HNh[:, sl], ALU.subtract).then_inc(s["hl"], 1)
                for u in range(3 * NCH):
                    c, kind = divmod(u, 3)
                    sl = slice(512 * c, 512 * c + 512)
                    after(ve, "evh", b * (3 * NCH) + (u + 1))
                    hi, lo = ((Qh, Ql), (Kh, Kl), (Vh, Vl))[kind]
                    if kind == 2:
                        ve.tensor_tensor(lo[:, sl], PS[:, u % 8, :], hi[:, sl], ALU.subtract).then_inc(s["evl"], 1)
                    else:
                        bias = SM[:, 2:3] if kind == 0 else vec(V_BK)
                        ve.scalar_tensor_tensor(lo[:, sl], PS[:, u % 8, :], bias, hi[:, sl], ALU.add, ALU.subtract).then_inc(s["evl"], 1)
                schedule(ve, b, unit)
                attn_out(b, NSB - 1, (NSB - 1) % 2)
                x1_out(b, NSB - 1, NSB // 2 - 1, (NSB - 1) % 2)

            ve.wait_ge(s_pz, 6)
            with ve.Fori(0, B) as b:
                for rb in range(NCH + 1):
                    if rb < NCH:
                        after(ve, "chi", b * NCH + (rb + 1))
                        w = (slice(None), slice(1 + 8 * rb, 9 + 8 * rb), slice(1, WW + 1))
                        ve.tensor_tensor(PDl[w], XC[:, rb % 4, :].rearrange("p (r w) -> p r w", w=WW), PDh[w],
                                         ALU.subtract).then_inc(s["clo"], 1)
                    if rb:
                        after(ve, "ye", b * NCH + rb)
                        bs = BS[:, bass.ds(b * NCH + (rb - 1), 1), :].rearrange("p a n -> p (a n)")
                        ve.bn_stats(bs, PS[:, (rb - 1) % 4, :]).then_inc(s["bs"], 1)
            lstep = [0]

            def l1(ins):
                lstep[0] += 1
                ins.then_inc(s["l1"], 1)
                after(ve, "l1", lstep[0])

            def norm(var_at, v0, gam, bet, sem_n):
                l1(ve.bn_aggr(SM[:, v0:v0 + 2], BS[:, :, :].rearrange("p a b -> p (a b)")))
                l1(ve.tensor_scalar(SM[:, v0 + 1:v0 + 2], SM[:, v0 + 1:v0 + 2], EPS, None, ALU.add))
                assert lstep[0] == var_at
                after(ve, "l1p", sem_n)
                l1(ve.tensor_tensor(SM[:, v0 + 3:v0 + 4], SM[:, v0 + 2:v0 + 3], gam, ALU.mult))
                l1(ve.tensor_tensor(SM[:, v0 + 4:v0 + 5], SM[:, v0:v0 + 1], SM[:, v0 + 3:v0 + 4], ALU.mult))
                l1(ve.tensor_tensor(SM[:, v0 + 5:v0 + 6], bet, SM[:, v0 + 4:v0 + 5], ALU.subtract))

            after(ve, "bs", B * NCH)
            norm(L1_VAR1, 10, vec(V_G1), vec(V_B1), 1)
            assert lstep[0] == L1_AB1
            with ve.Fori(0, B) as b:
                for rb in range(NCH + 1):
                    if rb < NCH:
                        n = b * NCH + rb
                        after(ve, "hA", n + 1)
                        after(ve, "of", b * NCH + (min(rb + 2, NCH) - NCH))
                        w = (slice(None), slice(1 + 8 * rb, 9 + 8 * rb), slice(1, WW + 1))
                        ht = HT[:, rb % 2, :].rearrange("p (r w) -> p r w", w=WW)
                        ve.tensor_copy(PDh[w], ht).then_inc(s["dsh"], 1)
                        after(ve, "dsh", n + 1)
                        ve.tensor_tensor(PDl[w], ht, PDh[w], ALU.subtract).then_inc(s["hp"], 1)
                    if rb:
                        after(ve, "xth", b * NCH + rb)
                        src = PS[:, 4 + (rb - 1) % 2, :].rearrange("p (t c) -> p t c", c=C)
                        xs = XS[:, (rb - 1) % 2, :, :]
                        ve.tensor_tensor(xs[:, :, C:2 * C], src, xs[:, :, 0:C], ALU.subtract).then_inc(s["xe"], 1)
            after(ve, "oc", B * NCH)
            boff = WF[:, W_BOFF:W_BOFF + NOFF][:, None, :].to_broadcast([128, B * 32, NOFF])
            l1(ve.tensor_tensor(OFF[:, :, :], OR[:, :, 0:NOFF], OR[:, :, NOFF:2 * NOFF], ALU.add))
            l1(ve.tensor_tensor(OFF[:, :, :], OFF[:, :, :], boff, ALU.add))
            yc = CN[:, K_YC:K_YC + TAPS][:, None, :].to_broadcast([128, B * 32, TAPS])
            l1(ve.tensor_tensor(PY[:, :, :], OFF[:, :, TAPS:NOFF], yc, ALU.add))
            l1(ve.tensor_reduce(SM[:, 28:29], OFF[:, :, 0:TAPS], AX.XY, ALU.max, apply_absolute_value=True))
            assert lstep[0] == L1_MAX
            after(ve, "fl", 1)
            l1(ve.tensor_reduce(SM[0:1, 29:30], PS[0:1, 6, 0:128], AX.X, ALU.max))
            l1(ve.tensor_scalar(SM[0:1, 30:31], SM[0:1, 29:30], REACH, None, ALU.is_gt))
            assert lstep[0] == L1_GT
            l1(ve.tensor_scalar(CNT[0:1, 0:1], SM[0:1, 30:31], 2.0 * SHIFTS, 1.0, ALU.mult, ALU.add))
            l1(ve.tensor_scalar(CNT[0:1, 1:2], SM[0:1, 30:31], -float(SHIFTS), float(SHIFTS), ALU.mult, ALU.add))
            after(ve, "fl", 2)
            l1(ve.tensor_scalar(SM[:, 31:32], PS[:, 7, 0:1], -float(WIN * SHIFTS), None, ALU.mult))
            assert lstep[0] == L1_FLAG
            after(ve, "fz", B)

            npass = ve.value_load(CNT[0:1, 0:1], min_val=1, max_val=2 * SHIFTS + 1)

            def sampled_lo(q, dx):
                after(ve, "xh", q * 3 + (dx + 1))
                ve.tensor_tensor(SOl[:, dx, :], PS[:, 3 + dx, 0:384], SOh[:, dx, :], ALU.subtract).then_inc(s["xl"], 1)

            with ve.Fori(0, npass) as n:
                with ve.Fori(0, B) as b:
                    for half in range(2):
                        hid, q0 = n * (2 * B) + b * 2 + half, n * 128 + b * 32 + half * HALF_TILES

                        def tile(q, tl, par, cur, prev, nxt):
                            for v in range(UNITS):
                                if cur:
                                    after(ve, "th", q * UNITS + (v + 1))
                                    ve.tensor_tensor(STl[:, v % 3, :], PS[:, v % 3, 0:384], STh[:, v % 3, :],
                                                     ALU.subtract).then_inc(s["tl"], 1)
                                if prev and v == 2:
                                    sampled_lo(q - 1, 2)
                                if nxt and v in (3, 6):
                                    product(ve, "pr", hid, q + 1, tl + 1, half, 1 - par, v // 3 - 1)
                                if cur and v in (5, 8):
                                    sampled_lo(q, v // 3 - 1)
                                if prev and v == 6:
                                    after(ve, "c2", q * 3)
                                    yz = Y[:, :, :].rearrange("p b n -> p (b n)")
                                    yz = yz[:, bass.ds(b * N + (tl + (half * HALF_TILES - 1)) * 128, 128)]
                                    ve.tensor_tensor(yz, PS[:, 7 - par, 0:128], yz, ALU.add).then_inc(s["z"], 1)

                        product(ve, "pr", hid, q0, 0, half, 0, 0)
                        product(ve, "pr", hid, q0, 0, half, 0, 1)
                        half_image(ve, q0, tile)
                after(ve, "hx", n * (2 * B) + 2 * B)
                ve.tensor_scalar(SM[:, 31:32], SM[:, 31:32], float(WIN), None, ALU.add).then_inc(s["dsh"], 1)
                after(ve, "dsh", n + (B * NCH + 1))
            after(ve, "z", npass * 128)
            for c in range(B * NCH):
                ins = ve.bn_stats(BS[:, c, :], Y[:, c // NCH, 512 * (c % NCH):512 * (c % NCH) + 512])
            ins.then_inc(s["bs"], 1)
            after(ve, "bs", B * NCH + 1)
            norm(L1_VAR2, 20, vec(V_G2), vec(V_B2), 2)
            assert lstep[0] == L1_AB2
            with ve.Fori(0, B) as b:
                for i in range(4):
                    ve.wait_ge(s_fx[i], b * 16 + 16)
                    zz = Y[:, bass.ds(b, 1), 1024 * i:1024 * i + 1024].rearrange("p a n -> p (a n)")
                    ve.scalar_tensor_tensor(FX[:, i, :], zz, SM[:, 23:24], FX[:, i, :], ALU.mult, ALU.add).then_inc(s["fr"], 1)

        @block.tensor
        def _(pe):
            def three(dst, lh, ll, rh, rl, start, stop):
                pe.matmul(dst, lh, rh, start=start, stop=False)
                pe.matmul(dst, lh, rl, start=False, stop=False)
                return pe.matmul(dst, ll, rh, start=False, stop=stop)

            pe.wait_ge(s_open, 1)
            pe.wait_ge(s_w, 16)
            pe.wait_ge(s_k, 16)
            pe.matmul(PS[:, 7, 0:1], WF[:, W_PROJ:W_PROJ + C], vec(V_BV), start=True, stop=True).then_inc(s_bp, 1)
            pe.wait_ge(s_ws, 1)

            def project(b, sb, par):
                after(pe, "ol", b * NSB + sb + 1)
                wp = slice(W_PROJ, W_PROJ + C)
                three(PS[:, 6 + par, SBQ:2 * SBQ], WH[:, wp], WL[:, wp], Oh[:, par, :], Ol[:, par, :], True, True).then_inc(s["pj"], 1)

            def values(b, sb, par, g):
                G = b * (NSB * GPS) + sb * GPS + g
                after(pe, "lo", G + 1)
                if g == 0:
                    after(pe, "x1", b * NSB + sb - 1)
                for mm in range(2):
                    m = slice(256 * g + 128 * mm, 256 * g + 128 * mm + 128)
                    r = slice(256 * mm, 256 * mm + 256)
                    last = three(PS[:, 6 + par, 0:SBQ], Vh[:, m], Vl[:, m], PTh[:, g % 4, r], PTl[:, g % 4, r],
                                 g == 0 and mm == 0, g == GPS - 1 and mm == 1)
                last.then_inc(s["av"], 1)

            def transposes(b, sb, par, g):
                G = b * (NSB * GPS) + sb * GPS + g
                if g % 4 == 0:
                    after(pe, "pp", b * (NSB * UPS) + sb * UPS + (4 + g // 4 + 1))
                after(pe, "lo", G - 1)
                for mm in range(2):
                    for i in range(2):
                        m = 256 * g + 128 * mm
                        last = pe.transpose(PS[:, 4 + g % 2, 256 * mm + 128 * i:256 * mm + 128 * i + 128],
                                            P[:, par, i, m:m + 128], ident)
                last.then_inc(s["T"], 1)

            def unit(b, sb, par, k, older, scores, late, vals):
                if scores:
                    i, j = divmod(k, 4)
                    U = b * (NSB * UPS) + sb * UPS + k
                    after(pe, "exp", U - 1)
                    qs = bass.ds(sb * SBQ + 128 * i, 128)
                    for e in range(2):
                        dst = PS[:, 2 * (k % 2) + e, :]
                        ks = slice(1024 * j + 512 * e, 1024 * j + 512 * e + 512)
                        last = three(dst, Qh[:, qs], Ql[:, qs], Kh[:, ks], Kl[:, ks], True, True)
                    last.then_inc(s["S"], 1)
                if vals is not None:
                    back, g0 = vals
                    for g in (g0, g0 + 1):
                        transposes(b, sb - back, (par + back) % 2, g)
                    if g0 or older is not None:
                        behind, g1 = (back, g0 - 2) if g0 else (back + 1, GPS - 2)
                        for g in (g1, g1 + 1):
                            values(b, sb - behind, (par + behind) % 2, g)
                    if g0 == 6 and older is not None:
                        project(b, sb - 2, par)

            with pe.Fori(0, B) as b:
                after(pe, "exp", b * NSB * UPS)
                after(pe, "lo", b * NSB * GPS)
                after(pe, "x1", b * NSB)
                after(pe, "gn", b * GN_STEPS + 3)
                pe.matmul(PS[:, 7, 0:2], CN[:, K_GRP:K_GRP + 128], SM[:, 4:6], start=True, stop=True).then_inc(s["gp"], 1)
                after(pe, "gn", b * GN_STEPS + 4)
                for u in range(3 * NCH):
                    c, kind = divmod(u, 3)
                    if kind == 0:
                        after(pe, "hl", b * NCH + (c + 1))
                    if u >= 8:
                        after(pe, "evl", b * (3 * NCH) + (u - 7))
                    cs = slice(512 * c, 512 * c + 512)
                    if kind < 2:
                        w = slice(kind * C, kind * C + C)
                        last = three(PS[:, u % 8, :], WH[:, w], WL[:, w], HNh[:, cs], HNl[:, cs], True, True)
                    else:
                        w = slice(2 * C, 3 * C)
                        for i in range(4):
                            m = slice(512 * c + 128 * i, 512 * c + 128 * i + 128)
                            last = three(PS[:, u % 8, 128 * i:128 * i + 128], HNh[:, m], HNl[:, m], WH[:, w], WL[:, w], True, True)
                    last.then_inc(s["qkv"], 1)
                after(pe, "evl", (b + 1) * (3 * NCH))
                schedule(pe, b, unit)
                for g in (GPS - 2, GPS - 1):
                    values(b, NSB - 1, (NSB - 1) % 2, g)
                project(b, NSB - 1, (NSB - 1) % 2)

            after(pe, "x1", B * NSB)
            with pe.Fori(0, B) as b:
                for rb in range(NCH):
                    after(pe, "clo", b * NCH + min(rb + 2, NCH))
                    after(pe, "ye", b * NCH + (rb - 3))
                    after(pe, "bs", b * NCH + (rb - 3))
                    for k in range(TAPS):
                        dx, dy = divmod(k, 3)
                        w = slice(W_1 + k * C, W_1 + k * C + C)
                        win = (slice(None), slice(8 * rb + dx, 8 * rb + dx + 8), slice(dy, dy + WW))
                        last = three(PS[:, rb % 4, :].rearrange("p (r w) -> p r w", w=WW), WH[:, w], WL[:, w], PDh[win], PDl[win], k == 0, k == TAPS - 1)
                    last.then_inc(s["cv"], 1)
            after(pe, "ye", B * NCH)
            after(pe, "bs", B * NCH)
            with pe.Fori(0, B) as b:
                for rb in range(NCH + 1):
                    if rb < NCH:
                        n = b * NCH + rb
                        after(pe, "hp", b * NCH + min(rb + 2, NCH))
                        after(pe, "oe", n - 1)
                        dst = PS[0:2 * NOFF, rb % 2, :].rearrange("p (r w) -> p r w", w=WW)
                        for k in range(TAPS):
                            dx, dy = divmod(k, 3)
                            win = (slice(None), slice(8 * rb + dx, 8 * rb + dx + 8), slice(dy, dy + WW))
                            pe.matmul(dst, OW1[:, k, :], PDh[win], start=k == 0, stop=False)
                            last = pe.matmul(dst, OW2[:, k, :], PDl[win], start=False, stop=k == TAPS - 1)
                        last.then_inc(s["of"], 1)
                        after(pe, "xe", n - 1)
                        for t in range(4):
                            tt = slice(128 * t, 128 * t + 128)
                            last = pe.transpose(PS[:, 4 + rb % 2, tt], HT[:, rb % 2, tt], ident)
                        last.then_inc(s["xt"], 1)
                    if rb:
                        n = b * NCH + (rb - 1)
                        after(pe, "oe", n + 1)
                        after(pe, "oc", n - 1)
                        for t in range(4):
                            tt = slice(128 * t, 128 * t + 128)
                            last = pe.transpose(PS[:, 2 + (rb - 1) % 2, tt], OE[:, (rb - 1) % 2, tt], ident)
                        last.then_inc(s["ot"], 1)
            after(pe, "l1", L1_MAX)
            pe.transpose(PS[0:1, 6, 0:128], SM[:, 28:29], ident).then_inc(s["fl"], 1)
            after(pe, "l1", L1_GT)
            pe.matmul(PS[:, 7, 0:1], CN[0:1, K_ONE:K_ONE + 128], SM[0:1, 30:31], start=True, stop=True).then_inc(s["fl"], 1)
            after(pe, "l1", L1_FLAG)
            npass = pe.value_load(CNT[0:1, 0:1], min_val=1, max_val=2 * SHIFTS + 1)

            def tr(q, par, v):
                dx, jb = divmod(v, BLOCKS)
                if v == 0 or v == BLOCKS:
                    after(pe, "pr", q * 2 + (dx + 1))
                if v == 2 * BLOCKS:
                    after(pe, "pq", q + 1)
                after(pe, "tl", q * UNITS + (v - 2))
                for dy in range(3):
                    last = pe.transpose(PS[:, v % 3, 128 * dy:128 * dy + 128],
                                        SS[:, par, 3 * dx + dy, 2 * jb:2 * jb + 2, :].rearrange("p j y -> p (j y)"), ident)
                last.then_inc(s["tt"], 1)

            def sample(q, tl, half, v):
                dx, jb = divmod(v, BLOCKS)
                after(pe, "tl", q * UNITS + (v + 1))
                if jb == 0:
                    after(pe, "xl", q * 3 + (dx - 2))
                w = bass.ds(tl + (dx // 2 + jb), 1)
                xh = XT[:, half, dx % 2, w, 0:C].rearrange("p a c -> p (a c)")
                xl = XT[:, half, dx % 2, w, C:2 * C].rearrange("p a c -> p (a c)")
                three(PS[:, 3 + dx, 0:384], xh, xl, STh[:, v % 3, :], STl[:, v % 3, :], jb == 0, jb == BLOCKS - 1).then_inc(s["mm"], 1)

            def conv2(q, par, dx):
                after(pe, "xl", q * 3 + (dx + 1))
                if dx == 0:
                    after(pe, "z", q - 1)
                for dy in range(3):
                    k = 3 * dx + dy
                    w = slice(W_2 + k * C, W_2 + k * C + C)
                    c = slice(128 * dy, 128 * dy + 128)
                    last = three(PS[:, 6 + par, 0:128], WH[:, w], WL[:, w], SOh[:, dx, c], SOl[:, dx, c], k == 0, k == TAPS - 1)
                last.then_inc(s["c2"], 1)

            with pe.Fori(0, npass) as n:
                with pe.Fori(0, B) as b:
                    for half in range(2):
                        def tile(q, tl, par, cur, prev, nxt):
                            pe.wait_ge(s_ld[half], (n * B + b + 1) * 64)
                            for v in range(UNITS):
                                if cur:
                                    tr(q, par, v)
                                if cur and v >= 2:
                                    sample(q, tl, half, v - 2)
                                if prev and v < 2:
                                    sample(q - 1, tl - 1, half, UNITS - 2 + v)
                                if prev and v in (1, 4):
                                    conv2(q - 1, 1 - par, v // 3 + 1)
                                if cur and v == 7:
                                    conv2(q, par, 0)

                        half_image(pe, n * 128 + b * 32 + half * HALF_TILES, tile)


def half_image(eng, q0, tile):
    tile(q0, 0, 0, True, False, True)
    with eng.Fori(0, HALF_TILES // 2 - 1) as u:
        for par in (1, 0):
            tl = u * 2 + (2 - par)
            tile(q0 + tl, tl, par, True, True, True)
    tile(q0 + (HALF_TILES - 1), HALF_TILES - 1, 1, True, True, False)
    tile(q0 + HALF_TILES, HALF_TILES, 0, False, True, False)


def schedule(eng, b, unit):
    def step(sb, par, older, static=None):
        for k in range(UPS):
            back = 1 if k >= LAG else 2
            g0 = 2 * ((k - LAG) % UPS)
            has = static is None or 0 <= static - back < NSB
            scores = static is None or static < NSB
            late = static is None or 0 < static * UPS + k <= NSB * UPS
            if scores or has or late:
                unit(b, sb, par, k, older, scores, late, (back, g0) if has else None)

    step(0, 0, None, 0)
    step(1, 1, None, 1)
    with eng.Fori(0, NSB // 2 - 1) as t:
        for par in range(2):
            step(t * 2 + (2 + par), par, t)
    step(NSB, 0, NSB // 2 - 1, NSB)
    step(NSB + 1, 1, NSB // 2 - 1, NSB + 1)


def kernel(**inputs):
    import numpy as np
    import concourse.bacc as bacc
    from concourse.bass_utils import run_bass_kernel_spmd as run

    a = {k: np.asarray(v) for k, v in inputs.items()}

    def taps(w):
        return w.reshape(w.shape[0], C, TAPS).transpose(1, 2, 0).reshape(C, -1)

    cols = [a["L0_conv_norm_w"], a["L0_conv_norm_b"], *a["L0_conv_qkv_b"].reshape(3, C), a["L0_conv_proj_b"],
            a["L1_conv_g1"], a["L1_conv_b1"], a["L1_conv_g2"], a["L1_conv_b2"]]
    weights = np.concatenate(
        [a["L0_conv_qkv_w"].T, a["L0_conv_proj_w"].T, taps(a["L1_conv_w1"]), taps(a["L1_conv_w2"]), taps(a["L1_conv_w_off"]),
         np.stack(cols, axis=1), np.broadcast_to(a["L1_conv_b_off"][None, :], (C, NOFF))], axis=1)
    p = np.arange(128)
    consts = np.zeros((128, K_ALL), np.float32)
    consts[:, K_ID:K_ID + 128] = np.eye(128)
    consts[:, K_GRP:K_GRP + 128] = (p[:, None] // NG_SIZE == p[None, :] // NG_SIZE) / NG_SIZE
    consts[:, K_ONE:K_ONE + 128] = 1.0
    consts[:, K_YC:K_YC + TAPS] = (p % WW)[:, None] + (np.arange(TAPS) % 3 - 1)[None, :]
    consts[:, K_JH:K_JH + WIN] = np.arange(WIN)[None, :] - (WIN // 2 - 1) - (p // WW)[:, None]
    consts[:, K_YI:K_YI + WW] = np.arange(WW)[None, :]
    arrays = {"x": np.ascontiguousarray(a["x"]), "weights": np.ascontiguousarray(weights), "consts": consts}

    nc = bacc.Bacc("TRN2", target_bir_lowering=False, num_devices=1)
    aps = {k: nc.dram_tensor(k, v.shape, F32, kind="ExternalInput").ap() for k, v in arrays.items()}
    out = nc.dram_tensor("out", (B, C, HH, WW), F32, kind="ExternalOutput").ap()
    build(nc, aps["x"], aps["weights"], aps["consts"], out)
    r = run(nc, [arrays], core_ids=[0])
    return r.results[0]["out"]
```

```python
import concourse.bass as bass
from concourse import mybir
from contextlib import ExitStack

F32 = mybir.dt.float32
F16 = mybir.dt.float16
I32 = mybir.dt.int32
ALU = mybir.AluOpType
ACT = mybir.ActivationFunctionType
AX = mybir.AxisListType

B, C, HH, WW = 4, 128, 64, 64
N = HH * WW
NG_SIZE = C // 32
EPS = 1e-5
NCH = N // 512
SBQ = 256
NSB = N // SBQ
UPS = 8
GPS = N // 256
LAG = 3
PSCALE = 2.0 ** 14
TAPS = 9
NOFF = 2 * TAPS
WIN = 6
BLOCKS = WIN // 2
UNITS = 3 * BLOCKS
REACH = float(WIN // 2 - 1)
SHIFTS = (HH + WIN - 1) // WIN
GAP = WIN * (SHIFTS + 1)
HALF_TILES = 16
XT_WINDOWS = 2 * HALF_TILES + WIN - 1
ROWS = 2 * WIN * SHIFTS + (B - 1) * (HH + GAP) + GAP + 32 + XT_WINDOWS
TOP = WIN // 2
OPEN = 32

W_QKV, W_PROJ = 0, 3 * C
W_1 = W_PROJ + C
W_2 = W_1 + TAPS * C
W_OFF = W_2 + TAPS * C
W_MM = W_OFF + TAPS * NOFF
V_NW, V_NB, V_BQ, V_BK, V_BV, V_BP, V_G1, V_B1, V_G2, V_B2 = range(W_MM, W_MM + 10)
W_BOFF = W_MM + 10
W_ALL = W_BOFF + NOFF

K_ID, K_GRP, K_ONE, K_YC = 0, 128, 256, 384
K_JH = K_YC + TAPS
K_YI = K_JH + WIN
K_ALL = K_YI + WW

GN_STEPS = 9
L1_VAR1, L1_AB1, L1_MAX, L1_GT, L1_FLAG, L1_VAR2, L1_AB2 = 2, 5, 9, 11, 14, 16, 19


def build(nc, x, weights, consts, out):
    x1_dram = nc.dram_tensor("x1_scratch", [B, C, N], F32, kind="Internal").ap()
    xt_dram = nc.dram_tensor("xt_scratch", [ROWS * WW, 2 * C], F16, kind="Internal").ap()
    out = out.rearrange("b c h w -> b c (h w)")
    x = x.rearrange("b c h w -> b c (h w)")

    ctx = ExitStack()
    with ctx:
        def sem(name):
            return ctx.enter_context(nc.semaphore(name))

        def sb_in(scope, name, shape, dt):
            return scope.enter_context(nc.sbuf_tensor(name, shape, dt))

        WF = sb_in(ctx, "weights_f32", [128, W_ALL], F32)
        WH = sb_in(ctx, "weights_hi", [128, W_MM], F16)
        WL = sb_in(ctx, "weights_lo", [128, W_MM], F16)
        CN = sb_in(ctx, "constants", [128, K_ALL], F32)
        OW1 = sb_in(ctx, "offset_w_hi_lo", [128, TAPS, 2 * NOFF], F16)
        OW2 = sb_in(ctx, "offset_w_hi_zero", [128, TAPS, 2 * NOFF], F16)
        SM = sb_in(ctx, "small", [128, 64], F32)
        ZT = sb_in(ctx, "zeros_f16", [128, 768], F16)
        CNT = sb_in(ctx, "pass_counts", [1, 2], I32)
        ident = CN[:, K_ID:K_ID + 128]

        l0 = ExitStack()
        XIN = sb_in(l0, "x_image", [128, N], F32)
        HNh = sb_in(l0, "h_hi", [128, N], F16)
        HNl = sb_in(l0, "h_lo", [128, N], F16)
        Qh = sb_in(l0, "q_hi", [128, N], F16)
        Ql = sb_in(l0, "q_lo", [128, N], F16)
        Kh = sb_in(l0, "k_hi", [128, N], F16)
        Kl = sb_in(l0, "k_lo", [128, N], F16)
        Vh = sb_in(l0, "vT_hi", [128, N], F16)
        Vl = sb_in(l0, "vT_lo", [128, N], F16)
        P = sb_in(l0, "probs", [128, 2, 2, N], F32)
        PTh = sb_in(l0, "probsT_hi", [128, 4, 512], F16)
        PTl = sb_in(l0, "probsT_lo", [128, 4, 512], F16)
        Oh = sb_in(l0, "attn_hi", [128, 2, SBQ], F16)
        Ol = sb_in(l0, "attn_lo", [128, 2, SBQ], F16)
        XR = sb_in(l0, "x_residual", [128, 2, SBQ], F32)
        XO = sb_in(l0, "x1_out", [128, 2, SBQ], F32)
        NM = sb_in(l0, "neg_max", [128, 2, 2, 4], F32)
        NMF = sb_in(l0, "neg_max_row", [128, 2, 2, 1], F32)
        LS = sb_in(l0, "chunk_sums", [128, 2, 2, 4], F32)
        AL = sb_in(l0, "chunk_rescale", [128, 2, 2, 4], F32)
        BE = sb_in(l0, "chunk_factor", [128, 2, 2, 4], F32)
        TS = sb_in(l0, "sum_scratch", [128, 2, 2, 6], F32)
        GATE = sb_in(l0, "pool_gate", [128, 4], F32)
        ST6 = sb_in(l0, "gn_stats", [128, NCH, 6], F32)
        l0.close()

        l1 = ExitStack()
        Y = sb_in(l1, "y1_then_z", [128, B, N], F32)
        OFF = sb_in(l1, "offsets", [128, B * 32, NOFF], F32)
        PY = sb_in(l1, "sample_cols", [128, B * 32, TAPS], F32)
        BS = sb_in(l1, "bn_stats", [128, B * NCH, 6], F32)
        XS = sb_in(l1, "xt_stage", [128, 2, 4, 2 * C], F16)
        l1a = ExitStack()
        XC = sb_in(l1a, "x1_rows", [128, 4, 512], F32)
        PDh = sb_in(l1a, "padded_hi", [128, HH + 2, WW + 2], F16)
        PDl = sb_in(l1a, "padded_lo", [128, HH + 2, WW + 2], F16)
        HT = sb_in(l1a, "h1_rows", [128, 4, 512], F32)
        OE = sb_in(l1a, "offset_rows", [128, 2, 512], F32)
        OR = sb_in(l1a, "offset_parts", [128, B * 32, 2 * NOFF], F32)
        l1a.close()
        l1b = ExitStack()
        XT = sb_in(l1b, "xt_windows", [128, 2, 2, (XT_WINDOWS + 1) // 2, 2 * C], F16)
        HX = sb_in(l1b, "row_hats", [128, 2, HALF_TILES * TAPS, WIN], F32)
        DD = sb_in(l1b, "col_distance", [128, 2, TAPS, WW], F32)
        HY = sb_in(l1b, "col_hats", [128, 2, TAPS, WW], F32)
        SS = sb_in(l1b, "interp", [128, 2, TAPS, WIN, WW], F32)
        STh = sb_in(l1b, "interpT_hi", [128, 3, 384], F16)
        STl = sb_in(l1b, "interpT_lo", [128, 3, 384], F16)
        SOh = sb_in(l1b, "sampled_hi", [128, 3, 384], F16)
        SOl = sb_in(l1b, "sampled_lo", [128, 3, 384], F16)
        l1b.close()
        l1c = ExitStack()
        FX = sb_in(l1c, "final", [128, 4 * B, N // 4], F32)
        l1c.close()
        l1.close()

        PS = ctx.enter_context(nc.psum_tensor("psum", [128, 8, 512], F32))

        s_w = sem("weights_loaded")
        s_k = sem("constants_loaded")
        s_zf = sem("zero_rows_stored")
        s_open = sem("opened")
        s_set = sem("setup_steps")
        s_wh = sem("weights_hi_ready")
        s_ws = sem("weights_ready")
        s_bp = sem("bias_product")
        s_pz = sem("pool_cleared")
        s_x = sem("image_loaded")
        s_xr = [sem(f"residual_loaded{i}") for i in range(2)]
        s_xo = [sem(f"x1_stored{i}") for i in range(2)]
        s_xc = [sem(f"rows_loaded{i}") for i in range(4)]
        s_xs = [sem(f"xt_stored{i}") for i in range(2)]
        s_ld = [sem(f"windows_loaded{i}") for i in range(2)]
        s_fx = [sem(f"final_loaded{i}") for i in range(B)]
        s_fo = sem("final_stored")

        names = dict(
            gn="gn_steps", gp="gn_product", rs="gn_rstd", h32="h_affine", hh="h_hi_ready", hl="h_lo_ready",
            qkv="qkv_product", evh="qkv_hi_ready", evl="qkv_lo_ready",
            S="scores", mx="chunk_max", exp="chunk_exp", nm="row_max", al="rescale", bc="sum_steps",
            be="factor", pp="probs_scaled", T="probs_transposed", hi="probsT_hi_ready", lo="probsT_lo_ready",
            av="values", oh="attn_hi_ready", ol="attn_lo_ready", pj="projected", x1="x1_ready",
            chi="rows_hi_ready", clo="rows_lo_ready", cv="conv1", ye="y1_ready", bs="y1_stats",
            hA="h1_ready", hp="h1_split", of="offset_conv", oe="offset_rows_ready", ot="offset_transposed",
            oc="offset_copied", xt="h1_transposed", xth="h1T_hi_ready", xe="h1T_ready",
            hd="row_distance", hb="row_abs", hx="row_hats_ready", pq="interp_part_ready", dd="distance_ready", ab="distance_abs", hy="col_hat_ready", pr="interp_ready",
            tt="interp_transposed", th="interpT_hi_ready", tl="interpT_lo_ready", mm="sampled",
            xh="sampled_hi_ready", xl="sampled_lo_ready", c2="conv2", z="z_added", dsh="shift_steps",
            l1="bn_steps", l1p="bn_rstd", fl="flag_product", fz="z_cleared", fr="final_sum", fa="final_relu")
        s = {k: sem(v) for k, v in names.items()}

        def after(eng, key, count):
            eng.wait_ge(s[key], count + OPEN)

        def stored(eng, slot_sem, n):
            eng.wait_ge(slot_sem, n * 16 + OPEN)

        def vec(i):
            return WF[:, i:i + 1]

        block = ctx.enter_context(nc.Block())

        def product(eng, key, hid, q, tl, half, par, dx):
            after(eng, "hx", hid + 1)
            after(eng, "hy", q + 1)
            after(eng, "tt", (q - 1) * UNITS)
            hy = HY[:, par, 3 * dx:3 * dx + 3, None, :].to_broadcast([128, 3, WIN, WW])
            hx = HX[:, half, bass.ds(tl * TAPS + 3 * dx, 3), :].rearrange("p k j -> p (k j)")
            eng.tensor_tensor(SS[:, par, 3 * dx:3 * dx + 3, :, :], hy, hx[:, :, None].to_broadcast([128, 3 * WIN, WW]),
                              ALU.mult).then_inc(s[key], 1)

        @block.sync
        def _(sp):
            sp.dma_start(WF[:, :], weights).then_inc(s_w, 16)
            sp.dma_start(CN[:, :], consts).then_inc(s_k, 16)
            sp.dma_start(XIN[:, :], x[0]).then_inc(s_x, 16)
            sp.wait_ge(s_open, 1)
            sp.wait_ge(s_pz, 1)
            for i in range(B + 1):
                r0 = i * (HH + GAP)
                dst = xt_dram[r0 * WW:(r0 + GAP) * WW, :].rearrange("(p a b) c -> p a (b c)", p=128, b=3)
                sp.dma_start(dst, ZT[:, None, :].to_broadcast([128, GAP * WW // 384, 768])).then_inc(s_zf, 16)

            def superblocks(b):
                with sp.Fori(0, NSB // 2) as t:
                    for par in range(2):
                        after(sp, "x1", b * NSB + t * 2 + (par - 1))
                        sp.dma_start(XR[:, par, :], x[b, :, bass.ds(t * (2 * SBQ) + par * SBQ, SBQ)]).then_inc(s_xr[par], 16)
                    for par in range(2):
                        after(sp, "x1", b * NSB + t * 2 + (par + 1))
                        sp.dma_start(x1_dram[b, :, bass.ds(t * (2 * SBQ) + par * SBQ, SBQ)], XO[:, par, :]).then_inc(s_xo[par], 16)

            with sp.Fori(0, B - 1) as b:
                after(sp, "hl", (b + 1) * NCH)
                sp.dma_start(XIN[:, :], x[b + 1]).then_inc(s_x, 16)
                superblocks(b)
            superblocks(B - 1)

            for par in range(2):
                stored(sp, s_xo[par], B * NSB // 2)
            with sp.Fori(0, B) as b:
                for rb in range(NCH):
                    after(sp, "clo", b * NCH + (rb - 3))
                    sp.dma_start(XC[:, rb % 4, :], x1_dram[b, :, 512 * rb:512 * rb + 512]).then_inc(s_xc[rb % 4], 16)
            with sp.Fori(0, B) as b:
                for rb in range(NCH):
                    after(sp, "xe", b * NCH + (rb + 1))
                    row = b * (HH + GAP) + (GAP + 8 * rb)
                    sp.dma_start(xt_dram[bass.ds(row * WW, 8 * WW), :].rearrange("(t p) c -> p t c", p=128),
                                 XS[:, rb % 2, :, :]).then_inc(s_xs[rb % 2], 16)
            for i in range(2):
                stored(sp, s_xs[i], B * NCH // 2)
            sp.wait_ge(s_zf, 16 * (B + 1))
            after(sp, "l1", L1_FLAG)
            npass = sp.value_load(CNT[0:1, 0:1], min_val=1, max_val=2 * SHIFTS + 1)
            first = sp.value_load(CNT[0:1, 1:2], min_val=0, max_val=SHIFTS)
            with sp.Fori(0, npass) as n:
                with sp.Fori(0, B) as b:
                    for half in range(2):
                        row = (n + first) * WIN + b * (HH + GAP) + (GAP - TOP + 32 * half - WIN * SHIFTS)
                        after(sp, "z", n * 128 + b * 32 + (half - 1) * HALF_TILES)
                        for odd in range(2):
                            for w0, w1 in ((0, 10), (10, XT_WINDOWS // 2 + 1 - odd)):
                                src = xt_dram[bass.ds((row + (odd + 2 * w0)) * WW, (w1 - w0) * 128), :]
                                sp.dma_start(XT[:, half, odd, w0:w1, :],
                                             src.rearrange("(w p) c -> p w c", p=128)).then_inc(s_ld[half], 16)
            for i in range(4 * B):
                if i == 0:
                    after(sp, "z", npass * 128 - HALF_TILES)
                if i == 4:
                    after(sp, "z", npass * 128)
                sp.dma_start(FX[:, i, :], x1_dram[i // 4, :, 1024 * (i % 4):1024 * (i % 4) + 1024]).then_inc(s_fx[i // 4], 16)
            for i in range(4 * B):
                after(sp, "fa", i + 1)
                sp.dma_start(out[i // 4, :, 1024 * (i % 4):1024 * (i % 4) + 1024], FX[:, i, :]).then_inc(s_fo, 16)
            sp.wait_ge(s_fo, 4 * B * 16)

        @block.gpsimd
        def _(po):
            for k in s:
                po.sem_inc(s[k], OPEN)
            for k in s_xo + s_xs:
                po.sem_inc(k, OPEN)
            po.sem_inc(s_open, 1)
            po.memset(ZT[:, :], 0.0).then_inc(s_pz, 1)
            po.memset(OW2[:, :, :], 0.0).then_inc(s_pz, 1)
            po.memset(SM[:, 0:1], -0.5).then_inc(s_pz, 1)
            po.memset(SM[:, 1:2], 1.0).then_inc(s_pz, 1)
            po.wait_ge(s_pz, 4)
            with po.Fori(0, B) as b:
                after(po, "gn", b * GN_STEPS + 6)
                po.tensor_tensor(SM[:, 8:9], SM[:, 7:8], SM[:, 0:1], ALU.pow).then_inc(s["rs"], 1)
                with po.Fori(0, NSB // 2) as t:
                    for par in range(2):
                        for i in range(2):
                            v = b * (2 * NSB) + t * 4 + (2 * par + i)
                            after(po, "pp", v * 4)
                            after(po, "be", v + 1)
                            po.tensor_tensor(GATE[:, 0:4], BE[:, par, i, :], BE[:, par, i, :], ALU.mult)
                            for j in range(4):
                                pj = P[:, par, i, 1024 * j:1024 * j + 1024]
                                po.tensor_scalar(pj, pj, BE[:, par, i, j:j + 1], PSCALE, ALU.mult, ALU.mult).then_inc(s["pp"], 1)
            after(po, "x1", B * NSB)
            after(po, "pj", B * NSB)
            po.memset(OE[:, :, :], 0.0)
            for t in (PDh, PDl):
                po.memset(t[:, 0, :], 0.0)
                po.memset(t[:, HH + 1, :], 0.0)
                po.memset(t[:, 1:HH + 1, 0:1], 0.0)
                po.memset(t[:, 1:HH + 1, WW + 1:WW + 2], 0.0).then_inc(s_pz, 1)
            after(po, "l1", L1_VAR1)
            po.tensor_tensor(SM[:, 12:13], SM[:, 11:12], SM[:, 0:1], ALU.pow).then_inc(s["l1p"], 1)
            after(po, "hA", B * NCH)
            for b in range(B):
                po.memset(Y[:, b, :], 0.0).then_inc(s["fz"], 1)
            after(po, "l1", L1_FLAG)
            npass = po.value_load(CNT[0:1, 0:1], min_val=1, max_val=2 * SHIFTS + 1)

            def distance(q, tile, par):
                after(po, "hy", q - 1)
                py = PY[:, bass.ds(tile, 1), :].rearrange("p a k -> p (a k)")
                po.tensor_tensor(DD[:, par, :, :], CN[:, K_YI:K_YI + WW][:, None, :].to_broadcast([128, TAPS, WW]),
                                 py[:, :, None].to_broadcast([128, TAPS, WW]), ALU.subtract).then_inc(s["dd"], 1)

            def products(hid, q, tl, half, par):
                for dx in (1, 2):
                    product(po, "pq", hid, q, tl, half, par, dx)

            def row_distance(half, t0):
                po.tensor_tensor(HX[:, half, :, :].rearrange("p (t k) j -> p t k j", k=TAPS),
                                 CN[:, K_JH:K_JH + WIN][:, None, None, :].to_broadcast([128, HALF_TILES, TAPS, WIN]),
                                 OFF[:, bass.ds(t0, HALF_TILES), 0:TAPS][:, :, :, None].to_broadcast([128, HALF_TILES, TAPS, WIN]),
                                 ALU.subtract).then_inc(s["hd"], 1)

            with po.Fori(0, npass) as n:
                after(po, "pr", n * 128)
                row_distance(0, 0)
                distance(n * 128, 0, 0)
                distance(n * 128 + 1, 1, 1)

                def half_tiles(b, half, last):
                    hid, t0 = n * (2 * B) + b * 2 + half, b * 32 + half * HALF_TILES
                    q0 = n * 128 + t0
                    with po.Fori(0, HALF_TILES // 2 - 1) as u:
                        for par in range(2):
                            tl = u * 2 + par
                            products(hid, q0 + tl, tl, half, par)
                            distance(q0 + (tl + 2), t0 + (tl + 2), par)
                    if not last:
                        after(po, "pr", q0)
                        row_distance(1 - half, t0 + HALF_TILES)
                    for par in range(2):
                        tl = HALF_TILES - 2 + par
                        products(hid, q0 + tl, tl, half, par)
                        if not last:
                            distance(q0 + (tl + 2), t0 + (tl + 2), par)

                halves(po, half_tiles)
            after(po, "l1", L1_VAR2)
            po.tensor_tensor(SM[:, 22:23], SM[:, 21:22], SM[:, 0:1], ALU.pow).then_inc(s["l1p"], 1)

        @block.scalar
        def _(act):
            act.wait_ge(s_open, 1)
            act.wait_ge(s_set, 1)
            act.activation(WH[:, :], WF[:, 0:W_MM], ACT.Copy).then_inc(s_wh, 1)

            def unit(b, sb, par, k, older, scores, late, values):
                if late:
                    par_, sb_ = (par, sb) if k else (1 - par, sb - 1)
                    i, j = divmod((k - 1) % UPS, 4)
                    U = b * (NSB * UPS) + sb * UPS + (k - 1)
                    after(act, "mx", U + 1)
                    after(act, "T", b * (NSB * GPS) + sb_ * GPS + (4 * j + 4 - 2 * GPS))
                    sc = PS[:, 2 * (j % 2):2 * (j % 2) + 2, :].rearrange("p a n -> p (a n)")
                    act.activation(P[:, par_, i, 1024 * j:1024 * j + 1024], sc, ACT.Exp, bias=NM[:, par_, i, j:j + 1],
                                   accum_out=LS[:, par_, i, j:j + 1]).then_inc(s["exp"], 1)
                    if j == 3:
                        V = b * (2 * NSB) + sb_ * 2 + i
                        after(act, "nm", V + 1)
                        act.activation(AL[:, par_, i, :], NM[:, par_, i, :], ACT.Exp, scale=-1.0,
                                       bias=NMF[:, par_, i, :]).then_inc(s["al"], 1)
                if values is not None:
                    back, g0 = values
                    for g in (g0, g0 + 1):
                        G = b * (NSB * GPS) + (sb - back) * GPS + g
                        after(act, "T", G + 1)
                        after(act, "av", G - 3)
                        act.activation(PTh[:, g % 4, :], PS[:, 4 + g % 2, :], ACT.Copy).then_inc(s["hi"], 1)
                    if g0 == 2 and older is not None:
                        attn_out(b, sb - 2, par)

            def attn_out(b, sb, par):
                after(act, "av", b * (NSB * GPS) + sb * GPS + GPS)
                act.activation(Oh[:, par, :], PS[:, 6 + par, 0:SBQ], ACT.Copy, scale=1.0 / PSCALE).then_inc(s["oh"], 1)

            def h_hi(b, c):
                if c == 0:
                    after(act, "qkv", b * 3 * NCH)
                after(act, "h32", b * NCH + (c + 1))
                act.activation(HNh[:, 512 * c:512 * c + 512], XIN[:, 512 * c:512 * c + 512], ACT.Copy).then_inc(s["hh"], 1)

            for c in range(NCH):
                h_hi(0, c)

            def image(b, more):
                after(act, "av", b * NSB * GPS)
                for u in range(3 * NCH):
                    c, kind = divmod(u, 3)
                    after(act, "qkv", b * (3 * NCH) + (u + 1))
                    dst = (Qh, Kh, Vh)[kind][:, 512 * c:512 * c + 512]
                    if kind == 2:
                        act.activation(dst, PS[:, u % 8, :], ACT.Copy).then_inc(s["evh"], 1)
                    else:
                        bias = SM[:, 2:3] if kind == 0 else vec(V_BK)
                        act.activation(dst, PS[:, u % 8, :], ACT.Identity, bias=bias).then_inc(s["evh"], 1)
                schedule(act, b, unit, next_norm(more, hi=lambda c: h_hi(b + 1, c)))
                attn_out(b, NSB - 1, (NSB - 1) % 2)

            with act.Fori(0, B - 1) as b:
                image(b, True)
            image(B - 1, False)

            after(act, "x1", B * NSB)
            after(act, "pj", B * NSB)
            act.wait_ge(s_pz, 6)
            def conv1_out(m, bank):
                after(act, "cv", m + 1)
                act.activation(Y[:, :, :].rearrange("p b n -> p (b n)")[:, bass.ds(m * 512, 512)], PS[:, bank, :],
                               ACT.Copy).then_inc(s["ye"], 1)

            def conv1_image(b, first):
                for rb in range(NCH):
                    act.wait_ge(s_xc[rb % 4], (b * 2 + (rb // 4 + 1)) * 16)
                    after(act, "cv", b * NCH + (min(rb + 2, NCH) - NCH))
                    act.activation(PDh[:, 1 + 8 * rb:9 + 8 * rb, 1:WW + 1],
                                   XC[:, rb % 4, :].rearrange("p (r w) -> p r w", w=WW), ACT.Copy).then_inc(s["chi"], 1)
                    if rb >= 2 or not first:
                        conv1_out(b * NCH + (rb - 2), (rb - 2) % 4)

            conv1_image(0, True)
            with act.Fori(1, B) as b:
                conv1_image(b, False)
            for m in (B * NCH - 2, B * NCH - 1):
                conv1_out(m, m % 4)
            after(act, "l1", L1_AB1)
            after(act, "ye", B * NCH)
            def h1_staged(m, par):
                after(act, "xt", m + 1)
                act.wait_ge(s_xs[par], (m - par) * 8 + OPEN)
                src = PS[:, 4 + par, :].rearrange("p (t c) -> p t c", c=C)
                act.activation(XS[:, par, :, 0:C], src, ACT.Copy).then_inc(s["xth"], 1)

            def offset_rows(m, par):
                after(act, "of", m + 1)
                after(act, "ot", m - 1)
                act.activation(OE[0:2 * NOFF, par, :], PS[0:2 * NOFF, par, :], ACT.Copy).then_inc(s["oe"], 1)

            def offset_pixels(m, par):
                after(act, "ot", m + 1)
                src = PS[:, 2 + par, :].rearrange("p (t k) -> p t k", t=4)[:, :, 0:2 * NOFF]
                act.activation(OR[:, bass.ds(m * 4, 4), :], src, ACT.Copy).then_inc(s["oc"], 1)

            def offset_image(b, rbs, first):
                for rb in rbs:
                    n = b * NCH + rb
                    if rb < NCH:
                        after(act, "hp", n - 3)
                        after(act, "xt", n - 3)
                        ys = Y[:, bass.ds(b, 1), 512 * rb:512 * rb + 512].rearrange("p a n -> p (a n)")
                        act.activation(HT[:, rb % 4, :], ys, ACT.Relu, scale=SM[:, 13:14], bias=SM[:, 15:16]).then_inc(s["hA"], 1)
                    if rb < NCH + 2 and (rb >= 2 or not first):
                        h1_staged(n - 2, rb % 2)
                    if rb < NCH + 3 and (rb >= 3 or not first):
                        offset_rows(n - 3, (rb + 1) % 2)
                    if rb >= 4 or not first:
                        offset_pixels(n - 4, rb % 2)

            offset_image(0, range(NCH), True)
            with act.Fori(1, B) as b:
                offset_image(b, range(NCH), False)
            offset_image(B - 1, range(NCH, NCH + 4), False)
            after(act, "l1", L1_FLAG)
            after(act, "xe", B * NCH)
            npass = act.value_load(CNT[0:1, 0:1], min_val=1, max_val=2 * SHIFTS + 1)

            def sampled(q, dx):
                after(act, "mm", q * UNITS + (BLOCKS * dx + BLOCKS))
                after(act, "c2", q * 3 + (dx - 2))
                act.activation(SOh[:, dx, :], PS[:, 3 + dx, 0:384], ACT.Copy).then_inc(s["xh"], 1)

            def col_abs(q, par):
                after(act, "dd", q + 1)
                act.activation(DD[:, par, :, :], DD[:, par, :, :], ACT.Abs).then_inc(s["ab"], 1)

            def col_hat(q, par):
                after(act, "ab", q + 1)
                after(act, "pr", q - 1)
                after(act, "pq", q * 2 - 2)
                act.activation(HY[:, par, :, :], DD[:, par, :, :], ACT.Relu, scale=-1.0, bias=1.0).then_inc(s["hy"], 1)

            def row_abs(hid, half):
                after(act, "hd", hid + 1)
                act.activation(HX[:, half, :, :], HX[:, half, :, :], ACT.Abs, bias=SM[:, 31:32]).then_inc(s["hb"], 1)

            def row_hat(hid, half):
                after(act, "hb", hid + 1)
                act.activation(HX[:, half, :, :], HX[:, half, :, :], ACT.Relu, scale=-1.0, bias=1.0).then_inc(s["hx"], 1)

            with act.Fori(0, npass) as n:
                after(act, "dsh", n + B * NCH)
                row_abs(n * (2 * B), 0)
                row_hat(n * (2 * B), 0)
                col_abs(n * 128, 0)
                col_hat(n * 128, 0)

                def tile(b, half, q, tl, par, cur, prev, nxt):
                    for v in range(UNITS):
                        if cur:
                            after(act, "tt", q * UNITS + (v + 1))
                            after(act, "mm", q * UNITS + (v - 2))
                            act.activation(STh[:, v % 3, :], PS[:, v % 3, 0:384], ACT.Copy).then_inc(s["th"], 1)
                        if nxt and v == 0:
                            col_abs(q + 1, 1 - par)
                        if nxt and v == 1:
                            col_hat(q + 1, 1 - par)
                        if nxt == SEAM and v in (0, 1):
                            (row_abs, row_hat)[v](n * (2 * B) + b * 2 + (half + 1), 1 - half)
                        if prev and v == 2:
                            sampled(q - 1, 2)
                        if cur and v in (5, 8):
                            sampled(q, v // 3 - 1)

                half_images(act, n, tile)
            after(act, "l1", L1_AB2)
            for i in range(4 * B):
                after(act, "fr", i + 1)
                act.activation(FX[:, i, :], FX[:, i, :], ACT.Relu, bias=SM[:, 25:26]).then_inc(s["fa"], 1)

        @block.vector
        def _(ve):
            step = [0]

            def link(ins):
                step[0] += 1
                ins.then_inc(s_set, 1)
                ve.wait_ge(s_set, step[0])

            ve.wait_ge(s_open, 1)
            ve.wait_ge(s_w, 16)
            link(ve.tensor_scalar(WF[:, 0:C], WF[:, 0:C], float(C) ** -0.5, None, ALU.mult))
            link(ve.tensor_scalar(SM[:, 2:3], vec(V_BQ), float(C) ** -0.5, None, ALU.mult))
            ve.wait_ge(s_wh, 1)
            link(ve.tensor_tensor(WL[:, :], WF[:, 0:W_MM], WH[:, :], ALU.subtract))
            ve.wait_ge(s_pz, 4)
            oh = WH[:, W_OFF:W_MM].rearrange("p (k o) -> p k o", k=TAPS)
            ol = WL[:, W_OFF:W_MM].rearrange("p (k o) -> p k o", k=TAPS)
            link(ve.tensor_copy(OW1[:, :, 0:NOFF], oh))
            link(ve.tensor_copy(OW1[:, :, NOFF:2 * NOFF], ol))
            link(ve.tensor_copy(OW2[:, :, 0:NOFF], oh))
            ve.wait_ge(s_bp, 1)
            ve.tensor_tensor(SM[:, 3:4], PS[:, 7, 0:1], vec(V_BP), ALU.add).then_inc(s_ws, 1)
            ve.wait_ge(s_ws, 1)

            def beta(b, sb, par, i):
                V = b * (2 * NSB) + sb * 2 + i
                after(ve, "al", V + 1)
                t = TS[:, par, i, :]
                ve.tensor_tensor(t[:, 0:4], AL[:, par, i, :], LS[:, par, i, :], ALU.mult).then_inc(s["bc"], 1)
                after(ve, "bc", V * 3 + 1)
                ve.reduce_sum(t[:, 4:5], t[:, 0:4], AX.X).then_inc(s["bc"], 1)
                after(ve, "bc", V * 3 + 2)
                ve.reciprocal(t[:, 5:6], t[:, 4:5]).then_inc(s["bc"], 1)
                after(ve, "bc", V * 3 + 3)
                ve.tensor_scalar(BE[:, par, i, :], AL[:, par, i, :], t[:, 5:6], None, ALU.mult).then_inc(s["be"], 1)

            def attn_out(b, sb, par):
                after(ve, "oh", b * NSB + sb + 1)
                ve.scalar_tensor_tensor(Ol[:, par, :], PS[:, 6 + par, 0:SBQ], 1.0 / PSCALE, Oh[:, par, :],
                                        ALU.mult, ALU.subtract).then_inc(s["ol"], 1)

            def x1_out(b, sb, half_sb, par):
                after(ve, "pj", b * NSB + sb + 1)
                ve.wait_ge(s_xr[par], (b * (NSB // 2) + half_sb + 1) * 16)
                stored(ve, s_xo[par], b * (NSB // 2) + half_sb)
                ve.scalar_tensor_tensor(XO[:, par, :], PS[:, 6 + par, SBQ:2 * SBQ], SM[:, 3:4], XR[:, par, :],
                                        ALU.add, ALU.add).then_inc(s["x1"], 1)

            def unit(b, sb, par, k, older, scores, late, values):
                if scores:
                    i, j = divmod(k, 4)
                    U = b * (NSB * UPS) + sb * UPS + k
                    after(ve, "S", U + 1)
                    sc = PS[:, 2 * (k % 2):2 * (k % 2) + 2, :].rearrange("p a n -> p (a n)")
                    ve.tensor_reduce(NM[:, par, i, j:j + 1], sc, AX.X, ALU.max, negate=True).then_inc(s["mx"], 1)
                    if j == 3:
                        after(ve, "mx", U + 1)
                        ve.tensor_reduce(NMF[:, par, i, :], NM[:, par, i, :], AX.X, ALU.min).then_inc(s["nm"], 1)
                if values is not None:
                    back, g0 = values
                    for g in (g0, g0 + 1):
                        G = b * (NSB * GPS) + (sb - back) * GPS + g
                        after(ve, "hi", G + 1)
                        ve.tensor_tensor(PTl[:, g % 4, :], PS[:, 4 + g % 2, :], PTh[:, g % 4, :], ALU.subtract).then_inc(s["lo"], 1)
                        if g == g0:
                            row_factors(b, sb, par, k, late)
                    if g0 == 2 and older is not None:
                        attn_out(b, sb - 2, par)
                    if g0 == 8 and older is not None:
                        x1_out(b, sb - 2, older, par)
                else:
                    row_factors(b, sb, par, k, late)

            def row_factors(b, sb, par, k, late):
                if late and k == 4:
                    beta(b, sb, par, 0)
                elif late and k == 0:
                    beta(b, sb - 1, 1 - par, 1)

            def gn_stats(b, c):
                if c == 0:
                    ve.wait_ge(s_x, b * 16 + 16)
                ins = ve.bn_stats(ST6[:, c, :], XIN[:, 512 * c:512 * c + 512])
                if c == NCH - 1:
                    ins.then_inc(s["gn"], 1)

            def gn_channel(b):
                g0 = b * GN_STEPS
                after(ve, "gn", g0 + 1)
                ve.tensor_copy(SM[:, 40:41], ST6[:, NCH - 1, 1:2])
                ve.bn_aggr(SM[:, 4:6], ST6[:, :, :].rearrange("p a b -> p (a b)")).then_inc(s["gn"], 1)
                after(ve, "gn", g0 + 2)
                ve.scalar_tensor_tensor(SM[:, 5:6], SM[:, 4:5], SM[:, 4:5], SM[:, 5:6], ALU.mult, ALU.add).then_inc(s["gn"], 1)

            def gn_group(b):
                g0 = b * GN_STEPS
                after(ve, "gp", b + 1)
                ve.tensor_copy(SM[:, 9:11], PS[:, 0, 0:2]).then_inc(s["gn"], 1)
                after(ve, "gn", g0 + 4)
                ve.scalar_tensor_tensor(SM[:, 6:7], SM[:, 9:10], SM[:, 9:10], SM[:, 10:11], ALU.mult, ALU.subtract).then_inc(s["gn"], 1)
                after(ve, "gn", g0 + 5)
                ve.tensor_scalar(SM[:, 7:8], SM[:, 6:7], -1.0, EPS, ALU.mult, ALU.add).then_inc(s["gn"], 1)

            def gn_affine(b):
                g0 = b * GN_STEPS
                after(ve, "rs", b + 1)
                ve.tensor_tensor(SM[:, 16:17], SM[:, 8:9], vec(V_NW), ALU.mult).then_inc(s["gn"], 1)
                after(ve, "gn", g0 + 7)
                ve.tensor_tensor(SM[:, 17:18], SM[:, 9:10], SM[:, 16:17], ALU.mult).then_inc(s["gn"], 1)
                after(ve, "gn", g0 + 8)
                ve.tensor_tensor(SM[:, 18:19], vec(V_NB), SM[:, 17:18], ALU.subtract).then_inc(s["gn"], 1)
                after(ve, "gn", g0 + 9)

            def h_affine(b, c):
                xc = XIN[:, 512 * c:512 * c + 512]
                ve.tensor_scalar(xc, xc, SM[:, 16:17], SM[:, 18:19], ALU.mult, ALU.add).then_inc(s["h32"], 1)

            def h_lo(b, c):
                after(ve, "hh", b * NCH + (c + 1))
                sl = slice(512 * c, 512 * c + 512)
                ve.tensor_tensor(HNl[:, sl], XIN[:, sl], HNh[:, sl], ALU.subtract).then_inc(s["hl"], 1)

            for c in range(NCH):
                gn_stats(0, c)
            gn_channel(0)
            gn_group(0)
            gn_affine(0)
            for c in range(NCH + 1):
                if c < NCH:
                    h_affine(0, c)
                if c:
                    h_lo(0, c - 1)

            def image(b, more):
                for u in range(3 * NCH):
                    c, kind = divmod(u, 3)
                    sl = slice(512 * c, 512 * c + 512)
                    after(ve, "evh", b * (3 * NCH) + (u + 1))
                    hi, lo = ((Qh, Ql), (Kh, Kl), (Vh, Vl))[kind]
                    if kind == 2:
                        ve.tensor_tensor(lo[:, sl], PS[:, u % 8, :], hi[:, sl], ALU.subtract).then_inc(s["evl"], 1)
                    else:
                        bias = SM[:, 2:3] if kind == 0 else vec(V_BK)
                        ve.scalar_tensor_tensor(lo[:, sl], PS[:, u % 8, :], bias, hi[:, sl], ALU.add, ALU.subtract).then_inc(s["evl"], 1)
                schedule(ve, b, unit, next_norm(more, stats=lambda c: gn_stats(b + 1, c), channel=lambda: gn_channel(b + 1),
                                                group=lambda: gn_group(b + 1), affine=lambda: gn_affine(b + 1),
                                                h32=lambda c: h_affine(b + 1, c), lo=lambda c: h_lo(b + 1, c)))
                attn_out(b, NSB - 1, (NSB - 1) % 2)
                x1_out(b, NSB - 1, NSB // 2 - 1, (NSB - 1) % 2)

            with ve.Fori(0, B - 1) as b:
                image(b, True)
            image(B - 1, False)

            ve.wait_ge(s_pz, 6)
            def conv1_stats(m, bank):
                after(ve, "ye", m + 1)
                bs = BS[:, bass.ds(m, 1), :].rearrange("p a n -> p (a n)")
                ve.bn_stats(bs, PS[:, bank, :]).then_inc(s["bs"], 1)

            def conv1_image(b, first):
                for rb in range(NCH):
                    after(ve, "chi", b * NCH + (rb + 1))
                    w = (slice(None), slice(1 + 8 * rb, 9 + 8 * rb), slice(1, WW + 1))
                    ve.tensor_tensor(PDl[w], XC[:, rb % 4, :].rearrange("p (r w) -> p r w", w=WW), PDh[w],
                                     ALU.subtract).then_inc(s["clo"], 1)
                    if rb >= 2 or not first:
                        conv1_stats(b * NCH + (rb - 2), (rb - 2) % 4)

            conv1_image(0, True)
            with ve.Fori(1, B) as b:
                conv1_image(b, False)
            for m in (B * NCH - 2, B * NCH - 1):
                conv1_stats(m, m % 4)
            lstep = [0]

            def l1(ins):
                lstep[0] += 1
                ins.then_inc(s["l1"], 1)
                after(ve, "l1", lstep[0])

            def norm(var_at, v0, gam, bet, sem_n):
                l1(ve.bn_aggr(SM[:, v0:v0 + 2], BS[:, :, :].rearrange("p a b -> p (a b)")))
                l1(ve.tensor_scalar(SM[:, v0 + 1:v0 + 2], SM[:, v0 + 1:v0 + 2], EPS, None, ALU.add))
                assert lstep[0] == var_at
                after(ve, "l1p", sem_n)
                l1(ve.tensor_tensor(SM[:, v0 + 3:v0 + 4], SM[:, v0 + 2:v0 + 3], gam, ALU.mult))
                l1(ve.tensor_tensor(SM[:, v0 + 4:v0 + 5], SM[:, v0:v0 + 1], SM[:, v0 + 3:v0 + 4], ALU.mult))
                l1(ve.tensor_tensor(SM[:, v0 + 5:v0 + 6], bet, SM[:, v0 + 4:v0 + 5], ALU.subtract))

            after(ve, "bs", B * NCH)
            norm(L1_VAR1, 10, vec(V_G1), vec(V_B1), 1)
            assert lstep[0] == L1_AB1
            def h1_split(b, rbs, first):
                for rb in rbs:
                    n = b * NCH + rb
                    if rb < NCH:
                        after(ve, "hA", n + 1)
                        after(ve, "of", b * NCH + (min(rb + 2, NCH) - NCH))
                        w = (slice(None), slice(1 + 8 * rb, 9 + 8 * rb), slice(1, WW + 1))
                        ht = HT[:, rb % 4, :].rearrange("p (r w) -> p r w", w=WW)
                        ve.tensor_copy(PDh[w], ht).then_inc(s["dsh"], 1)
                        after(ve, "dsh", n + 1)
                        ve.tensor_tensor(PDl[w], ht, PDh[w], ALU.subtract).then_inc(s["hp"], 1)
                    if rb >= 2 or not first:
                        after(ve, "xth", n - 1)
                        src = PS[:, 4 + rb % 2, :].rearrange("p (t c) -> p t c", c=C)
                        xs = XS[:, rb % 2, :, :]
                        ve.tensor_tensor(xs[:, :, C:2 * C], src, xs[:, :, 0:C], ALU.subtract).then_inc(s["xe"], 1)

            h1_split(0, range(NCH), True)
            with ve.Fori(1, B) as b:
                h1_split(b, range(NCH), False)
            h1_split(B - 1, range(NCH, NCH + 2), False)
            after(ve, "oc", B * NCH)
            boff = WF[:, W_BOFF:W_BOFF + NOFF][:, None, :].to_broadcast([128, B * 32, NOFF])
            l1(ve.tensor_tensor(OFF[:, :, :], OR[:, :, 0:NOFF], OR[:, :, NOFF:2 * NOFF], ALU.add))
            l1(ve.tensor_tensor(OFF[:, :, :], OFF[:, :, :], boff, ALU.add))
            yc = CN[:, K_YC:K_YC + TAPS][:, None, :].to_broadcast([128, B * 32, TAPS])
            l1(ve.tensor_tensor(PY[:, :, :], OFF[:, :, TAPS:NOFF], yc, ALU.add))
            l1(ve.tensor_reduce(SM[:, 28:29], OFF[:, :, 0:TAPS], AX.XY, ALU.max, apply_absolute_value=True))
            assert lstep[0] == L1_MAX
            after(ve, "fl", 1)
            l1(ve.tensor_reduce(SM[0:1, 29:30], PS[0:1, 6, 0:128], AX.X, ALU.max))
            l1(ve.tensor_scalar(SM[0:1, 30:31], SM[0:1, 29:30], REACH, None, ALU.is_gt))
            assert lstep[0] == L1_GT
            l1(ve.tensor_scalar(CNT[0:1, 0:1], SM[0:1, 30:31], 2.0 * SHIFTS, 1.0, ALU.mult, ALU.add))
            l1(ve.tensor_scalar(CNT[0:1, 1:2], SM[0:1, 30:31], -float(SHIFTS), float(SHIFTS), ALU.mult, ALU.add))
            after(ve, "fl", 2)
            l1(ve.tensor_scalar(SM[:, 31:32], PS[:, 7, 0:1], -float(WIN * SHIFTS), None, ALU.mult))
            assert lstep[0] == L1_FLAG
            after(ve, "fz", B)

            npass = ve.value_load(CNT[0:1, 0:1], min_val=1, max_val=2 * SHIFTS + 1)

            def sampled_lo(q, dx):
                after(ve, "xh", q * 3 + (dx + 1))
                ve.tensor_tensor(SOl[:, dx, :], PS[:, 3 + dx, 0:384], SOh[:, dx, :], ALU.subtract).then_inc(s["xl"], 1)

            yflat = Y[:, :, :].rearrange("p b n -> p (b n)")
            with ve.Fori(0, npass) as n:
                def z_stats(chunk, tiles):
                    after(ve, "z", n * 128 + tiles)
                    bs = BS[:, bass.ds(chunk, 1), :].rearrange("p a n -> p (a n)")
                    ve.bn_stats(bs, yflat[:, bass.ds(chunk * 512, 512)]).then_inc(s["bs"], 1)

                def tile(b, half, q, tl, par, cur, prev, nxt):
                    t0 = b * 32 + half * HALF_TILES
                    c0 = b * NCH + half * (NCH // 2)
                    for v in range(UNITS):
                        if cur:
                            after(ve, "th", q * UNITS + (v + 1))
                            ve.tensor_tensor(STl[:, v % 3, :], PS[:, v % 3, 0:384], STh[:, v % 3, :],
                                             ALU.subtract).then_inc(s["tl"], 1)
                        if prev and v == 2:
                            sampled_lo(q - 1, 2)
                        if nxt and v == 4:
                            hid = n * (2 * B) + b * 2 + half
                            if nxt == SEAM:
                                product(ve, "pr", hid + 1, q + 1, 0, 1 - half, 1 - par, 0)
                            else:
                                product(ve, "pr", hid, q + 1, tl + 1, half, 1 - par, 0)
                        if cur and v in (5, 8):
                            sampled_lo(q, v // 3 - 1)
                        if prev and v == 6:
                            after(ve, "c2", q * 3)
                            yz = yflat[:, bass.ds((t0 + (tl - 1)) * 128, 128)]
                            ve.tensor_tensor(yz, PS[:, 7 - par, 0:128], yz, ALU.add).then_inc(s["z"], 1)
                        if nxt != True and cur and v in (1, 4, 7):
                            z_stats(c0 + v // 3, t0 + 4 * (v // 3 + 1))
                        if prev == SEAM and v == 8:
                            behind = (c0, t0) if cur else (c0 + NCH // 2, t0 + HALF_TILES)
                            z_stats(behind[0] - 1, behind[1])

                product(ve, "pr", n * (2 * B), n * 128, 0, 0, 0, 0)
                half_images(ve, n, tile)
                after(ve, "hx", n * (2 * B) + 2 * B)
                ve.tensor_scalar(SM[:, 31:32], SM[:, 31:32], float(WIN), None, ALU.add).then_inc(s["dsh"], 1)
                after(ve, "dsh", n + (B * NCH + 1))
            after(ve, "bs", (npass + 1) * (B * NCH))
            ve.tensor_copy(SM[:, 41:42], BS[:, B * NCH - 1, 1:2])
            norm(L1_VAR2, 20, vec(V_G2), vec(V_B2), 2)
            assert lstep[0] == L1_AB2
            for i in range(4 * B):
                ve.wait_ge(s_fx[i // 4], 64)
                ve.scalar_tensor_tensor(FX[:, i, :], Y[:, i // 4, 1024 * (i % 4):1024 * (i % 4) + 1024], SM[:, 23:24],
                                        FX[:, i, :], ALU.mult, ALU.add).then_inc(s["fr"], 1)

        @block.tensor
        def _(pe):
            def three(dst, lh, ll, rh, rl, start, stop):
                pe.matmul(dst, lh, rh, start=start, stop=False)
                pe.matmul(dst, lh, rl, start=False, stop=False)
                return pe.matmul(dst, ll, rh, start=False, stop=stop)

            pe.wait_ge(s_open, 1)
            pe.wait_ge(s_w, 16)
            pe.wait_ge(s_k, 16)
            pe.matmul(PS[:, 7, 0:1], WF[:, W_PROJ:W_PROJ + C], vec(V_BV), start=True, stop=True).then_inc(s_bp, 1)
            pe.wait_ge(s_ws, 1)

            def project(b, sb, par):
                after(pe, "ol", b * NSB + sb + 1)
                wp = slice(W_PROJ, W_PROJ + C)
                three(PS[:, 6 + par, SBQ:2 * SBQ], WH[:, wp], WL[:, wp], Oh[:, par, :], Ol[:, par, :], True, True).then_inc(s["pj"], 1)

            def values(b, sb, par, g):
                G = b * (NSB * GPS) + sb * GPS + g
                after(pe, "lo", G + 1)
                if g == 0:
                    after(pe, "x1", b * NSB + sb - 1)
                for mm in range(2):
                    m = slice(256 * g + 128 * mm, 256 * g + 128 * mm + 128)
                    r = slice(256 * mm, 256 * mm + 256)
                    last = three(PS[:, 6 + par, 0:SBQ], Vh[:, m], Vl[:, m], PTh[:, g % 4, r], PTl[:, g % 4, r],
                                 g == 0 and mm == 0, g == GPS - 1 and mm == 1)
                last.then_inc(s["av"], 1)

            def transposes(b, sb, par, g):
                G = b * (NSB * GPS) + sb * GPS + g
                if g % 4 == 0:
                    after(pe, "pp", b * (NSB * UPS) + sb * UPS + (4 + g // 4 + 1))
                after(pe, "lo", G - 1)
                for mm in range(2):
                    for i in range(2):
                        m = 256 * g + 128 * mm
                        last = pe.transpose(PS[:, 4 + g % 2, 256 * mm + 128 * i:256 * mm + 128 * i + 128],
                                            P[:, par, i, m:m + 128], ident)
                last.then_inc(s["T"], 1)

            def unit(b, sb, par, k, older, scores, late, vals):
                if scores:
                    i, j = divmod(k, 4)
                    U = b * (NSB * UPS) + sb * UPS + k
                    after(pe, "exp", U - 1)
                    qs = bass.ds(sb * SBQ + 128 * i, 128)
                    for e in range(2):
                        dst = PS[:, 2 * (k % 2) + e, :]
                        ks = slice(1024 * j + 512 * e, 1024 * j + 512 * e + 512)
                        last = three(dst, Qh[:, qs], Ql[:, qs], Kh[:, ks], Kl[:, ks], True, True)
                    last.then_inc(s["S"], 1)
                if vals is not None:
                    back, g0 = vals
                    for g in (g0, g0 + 1):
                        transposes(b, sb - back, (par + back) % 2, g)
                    if g0 or older is not None:
                        behind, g1 = (back, g0 - 2) if g0 else (back + 1, GPS - 2)
                        for g in (g1, g1 + 1):
                            values(b, sb - behind, (par + behind) % 2, g)
                    if g0 == 6 and older is not None:
                        project(b, sb - 2, par)

            def group_means(b):
                after(pe, "exp", b * NSB * UPS)
                after(pe, "gn", b * GN_STEPS + 3)
                pe.matmul(PS[:, 0, 0:2], CN[:, K_GRP:K_GRP + 128], SM[:, 4:6], start=True, stop=True).then_inc(s["gp"], 1)

            group_means(0)

            def image(b, more):
                after(pe, "gn", b * GN_STEPS + 4)
                for u in range(3 * NCH):
                    c, kind = divmod(u, 3)
                    if u == 4:
                        after(pe, "lo", b * NSB * GPS)
                    if u == 6:
                        after(pe, "x1", b * NSB)
                    if kind == 0:
                        after(pe, "hl", b * NCH + (c + 1))
                    if u >= 8:
                        after(pe, "evl", b * (3 * NCH) + (u - 7))
                    cs = slice(512 * c, 512 * c + 512)
                    if kind < 2:
                        w = slice(kind * C, kind * C + C)
                        last = three(PS[:, u % 8, :], WH[:, w], WL[:, w], HNh[:, cs], HNl[:, cs], True, True)
                    else:
                        w = slice(2 * C, 3 * C)
                        for i in range(4):
                            m = slice(512 * c + 128 * i, 512 * c + 128 * i + 128)
                            last = three(PS[:, u % 8, 128 * i:128 * i + 128], HNh[:, m], HNl[:, m], WH[:, w], WL[:, w], True, True)
                    last.then_inc(s["qkv"], 1)
                after(pe, "evl", (b + 1) * (3 * NCH))
                schedule(pe, b, unit, next_norm(more, means=lambda: group_means(b + 1)))
                for g in (GPS - 2, GPS - 1):
                    values(b, NSB - 1, (NSB - 1) % 2, g)
                project(b, NSB - 1, (NSB - 1) % 2)

            with pe.Fori(0, B - 1) as b:
                image(b, True)
            image(B - 1, False)

            after(pe, "x1", B * NSB)
            with pe.Fori(0, B) as b:
                for rb in range(NCH):
                    after(pe, "clo", b * NCH + min(rb + 2, NCH))
                    after(pe, "ye", b * NCH + (rb - 3))
                    after(pe, "bs", b * NCH + (rb - 3))
                    for k in range(TAPS):
                        dx, dy = divmod(k, 3)
                        w = slice(W_1 + k * C, W_1 + k * C + C)
                        win = (slice(None), slice(8 * rb + dx, 8 * rb + dx + 8), slice(dy, dy + WW))
                        last = three(PS[:, rb % 4, :].rearrange("p (r w) -> p r w", w=WW), WH[:, w], WL[:, w], PDh[win], PDl[win], k == 0, k == TAPS - 1)
                    last.then_inc(s["cv"], 1)
            after(pe, "ye", B * NCH)
            after(pe, "bs", B * NCH)
            def offset_image(b, rbs, first):
                for rb in rbs:
                    n = b * NCH + rb
                    if rb < NCH:
                        after(pe, "hA", n + 1)
                        after(pe, "xe", n - 1)
                        for t in range(4):
                            tt = slice(128 * t, 128 * t + 128)
                            last = pe.transpose(PS[:, 4 + rb % 2, tt], HT[:, rb % 4, tt], ident)
                        last.then_inc(s["xt"], 1)
                        after(pe, "hp", b * NCH + min(rb + 2, NCH))
                        after(pe, "oe", n - 1)
                        dst = PS[0:2 * NOFF, rb % 2, :].rearrange("p (r w) -> p r w", w=WW)
                        for k in range(TAPS):
                            dx, dy = divmod(k, 3)
                            win = (slice(None), slice(8 * rb + dx, 8 * rb + dx + 8), slice(dy, dy + WW))
                            pe.matmul(dst, OW1[:, k, :], PDh[win], start=k == 0, stop=False)
                            last = pe.matmul(dst, OW2[:, k, :], PDl[win], start=False, stop=k == TAPS - 1)
                        last.then_inc(s["of"], 1)
                    if rb >= 2 or not first:
                        after(pe, "oe", n - 1)
                        after(pe, "oc", n - 3)
                        for t in range(4):
                            tt = slice(128 * t, 128 * t + 128)
                            last = pe.transpose(PS[:, 2 + rb % 2, tt], OE[:, rb % 2, tt], ident)
                        last.then_inc(s["ot"], 1)

            offset_image(0, range(NCH), True)
            with pe.Fori(1, B) as b:
                offset_image(b, range(NCH), False)
            offset_image(B - 1, range(NCH, NCH + 2), False)
            after(pe, "l1", L1_MAX)
            pe.transpose(PS[0:1, 6, 0:128], SM[:, 28:29], ident).then_inc(s["fl"], 1)
            after(pe, "l1", L1_GT)
            pe.matmul(PS[:, 7, 0:1], CN[0:1, K_ONE:K_ONE + 128], SM[0:1, 30:31], start=True, stop=True).then_inc(s["fl"], 1)
            after(pe, "l1", L1_FLAG)
            npass = pe.value_load(CNT[0:1, 0:1], min_val=1, max_val=2 * SHIFTS + 1)

            def tr(q, par, v):
                dx, jb = divmod(v, BLOCKS)
                if v == 0:
                    after(pe, "pr", q + 1)
                elif jb == 0:
                    after(pe, "pq", q * 2 + dx)
                after(pe, "tl", q * UNITS + (v - 2))
                for dy in range(3):
                    last = pe.transpose(PS[:, v % 3, 128 * dy:128 * dy + 128],
                                        SS[:, par, 3 * dx + dy, 2 * jb:2 * jb + 2, :].rearrange("p j y -> p (j y)"), ident)
                last.then_inc(s["tt"], 1)

            def sample(q, tl, half, v):
                dx, jb = divmod(v, BLOCKS)
                after(pe, "tl", q * UNITS + (v + 1))
                if jb == 0:
                    after(pe, "xl", q * 3 + (dx - 2))
                w = bass.ds(tl + (dx // 2 + jb), 1)
                xh = XT[:, half, dx % 2, w, 0:C].rearrange("p a c -> p (a c)")
                xl = XT[:, half, dx % 2, w, C:2 * C].rearrange("p a c -> p (a c)")
                three(PS[:, 3 + dx, 0:384], xh, xl, STh[:, v % 3, :], STl[:, v % 3, :], jb == 0, jb == BLOCKS - 1).then_inc(s["mm"], 1)

            def conv2(q, par, dx):
                after(pe, "xl", q * 3 + (dx + 1))
                if dx == 0:
                    after(pe, "z", q - 1)
                for dy in range(3):
                    k = 3 * dx + dy
                    w = slice(W_2 + k * C, W_2 + k * C + C)
                    c = slice(128 * dy, 128 * dy + 128)
                    last = three(PS[:, 6 + par, 0:128], WH[:, w], WL[:, w], SOh[:, dx, c], SOl[:, dx, c], k == 0, k == TAPS - 1)
                last.then_inc(s["c2"], 1)

            with pe.Fori(0, npass) as n:
                def tile(b, half, q, tl, par, cur, prev, nxt):
                    if cur:
                        pe.wait_ge(s_ld[half], (n * B + b + 1) * 64)
                    before = (HALF_TILES - 1, 1 - half) if prev == SEAM and cur else (tl - 1, half)
                    for v in range(UNITS):
                        if cur:
                            tr(q, par, v)
                        if cur and v >= 2:
                            sample(q, tl, half, v - 2)
                        if prev and v < 2:
                            sample(q - 1, *before, UNITS - 2 + v)
                        if prev and v in (1, 4):
                            conv2(q - 1, 1 - par, v // 3 + 1)
                        if cur and v == 7:
                            conv2(q, par, 0)

                half_images(pe, n, tile)


SEAM = 2


def halves(eng, half_tiles):
    with eng.Fori(0, B - 1) as b:
        half_tiles(b, 0, False)
        half_tiles(b, 1, False)
    half_tiles(B - 1, 0, False)
    half_tiles(B - 1, 1, True)


def half_images(eng, n, tile):
    tile(0, 0, n * 128, 0, 0, True, False, True)

    def half_tiles(b, half, last):
        q0 = n * 128 + b * 32 + half * HALF_TILES
        with eng.Fori(0, HALF_TILES // 2 - 1) as u:
            for par in (1, 0):
                tl = u * 2 + (2 - par)
                tile(b, half, q0 + tl, tl, par, True, True, True)
        tile(b, half, q0 + (HALF_TILES - 1), HALF_TILES - 1, 1, True, True, False if last else SEAM)
        if last:
            tile(b, half, q0 + HALF_TILES, HALF_TILES, 0, False, SEAM, False)
        else:
            tile(b + half, 1 - half, q0 + HALF_TILES, 0, 0, True, SEAM, True)

    halves(eng, half_tiles)


def next_norm(more, **steps):
    def at(static, k):
        if not more:
            return
        if static == 1 and k >= LAG and "stats" in steps:
            for c in range((k - LAG) * NCH // (UPS - LAG), (k - LAG + 1) * NCH // (UPS - LAG)):
                steps["stats"](c)
        when = {1: "channel", 2: "means", 3: "group", 4: "affine"}
        if static == NSB and when.get(k) in steps:
            steps[when[k]]()
        u = k if static == NSB else UPS + k if static == NSB + 1 else -1
        for name, first in (("h32", 5), ("hi", 6), ("lo", 7)):
            if 0 <= 2 * (u - first) < NCH and name in steps:
                for c in (2 * (u - first), 2 * (u - first) + 1):
                    steps[name](c)

    return at


def schedule(eng, b, unit, extra):
    def step(sb, par, older, static=None):
        for k in range(UPS):
            back = 1 if k >= LAG else 2
            g0 = 2 * ((k - LAG) % UPS)
            has = static is None or 0 <= static - back < NSB
            scores = static is None or static < NSB
            late = static is None or 0 < static * UPS + k <= NSB * UPS
            if scores or has or late:
                unit(b, sb, par, k, older, scores, late, (back, g0) if has else None)
            if static is not None:
                extra(static, k)

    step(0, 0, None, 0)
    step(1, 1, None, 1)
    with eng.Fori(0, NSB // 2 - 1) as t:
        for par in range(2):
            step(t * 2 + (2 + par), par, t)
    step(NSB, 0, NSB // 2 - 1, NSB)
    step(NSB + 1, 1, NSB // 2 - 1, NSB + 1)


def kernel(**inputs):
    import numpy as np
    import concourse.bacc as bacc
    from concourse.bass_utils import run_bass_kernel_spmd as run

    a = {k: np.asarray(v) for k, v in inputs.items()}

    def taps(w):
        return w.reshape(w.shape[0], C, TAPS).transpose(1, 2, 0).reshape(C, -1)

    cols = [a["L0_conv_norm_w"], a["L0_conv_norm_b"], *a["L0_conv_qkv_b"].reshape(3, C), a["L0_conv_proj_b"],
            a["L1_conv_g1"], a["L1_conv_b1"], a["L1_conv_g2"], a["L1_conv_b2"]]
    weights = np.concatenate(
        [a["L0_conv_qkv_w"].T, a["L0_conv_proj_w"].T, taps(a["L1_conv_w1"]), taps(a["L1_conv_w2"]), taps(a["L1_conv_w_off"]),
         np.stack(cols, axis=1), np.broadcast_to(a["L1_conv_b_off"][None, :], (C, NOFF))], axis=1)
    p = np.arange(128)
    consts = np.zeros((128, K_ALL), np.float32)
    consts[:, K_ID:K_ID + 128] = np.eye(128)
    consts[:, K_GRP:K_GRP + 128] = (p[:, None] // NG_SIZE == p[None, :] // NG_SIZE) / NG_SIZE
    consts[:, K_ONE:K_ONE + 128] = 1.0
    consts[:, K_YC:K_YC + TAPS] = (p % WW)[:, None] + (np.arange(TAPS) % 3 - 1)[None, :]
    consts[:, K_JH:K_JH + WIN] = np.arange(WIN)[None, :] - (WIN // 2 - 1) - (p // WW)[:, None]
    consts[:, K_YI:K_YI + WW] = np.arange(WW)[None, :]
    arrays = {"x": np.ascontiguousarray(a["x"]), "weights": np.ascontiguousarray(weights), "consts": consts}

    nc = bacc.Bacc("TRN2", target_bir_lowering=False, num_devices=1)
    aps = {k: nc.dram_tensor(k, v.shape, F32, kind="ExternalInput").ap() for k, v in arrays.items()}
    out = nc.dram_tensor("out", (B, C, HH, WW), F32, kind="ExternalOutput").ap()
    build(nc, aps["x"], aps["weights"], aps["consts"], out)
    r = run(nc, [arrays], core_ids=[0])
    return r.results[0]["out"]
```
